# Optimizing a Trainium2 kernel written in Bass

```python
import numpy as np
import jax
import jax.numpy as jnp

def _softmax(x, axis=-1):
    return jax.nn.softmax(x, axis=axis)

def _gelu(x):
    return jax.nn.gelu(x, approximate=True)

def _silu(x):
    return jax.nn.silu(x)

def _sigmoid(x):
    return jax.nn.sigmoid(x)

def _layernorm(x, axis=-1, eps=1e-05):
    m = jnp.mean(x, axis=axis, keepdims=True)
    v = jnp.var(x, axis=axis, keepdims=True)
    return (x - m) / jnp.sqrt(v + eps)

def _scatter_add(tgt, idx, src, axis=0):
    return tgt.at[idx].add(src)

def _segment_sum(src, seg, n):
    return jax.ops.segment_sum(src, seg, n)
kernel_name = 'mk_gnn_ffn_d1_gnn_r8_3840d2'

def setup_inputs(seed: int=0):
    np.random.seed(seed)
    _w = jnp.asarray

    def _rec_inputs():
        import jax
        import jax.numpy as jnp
        _gk = jax.random.key(seed)
        x = -7.329e-05 + 0.9999 * jax.random.normal(jax.random.fold_in(_gk, 1), (1250, 512), jnp.float32)
        _s = jax.random.randint(jax.random.fold_in(_gk, 2), (20000,), 0, 1250, jnp.int32)
        _d = jax.random.randint(jax.random.fold_in(_gk, 3), (20000,), 0, 1250, jnp.int32)
        _loop = jnp.arange(1250, dtype=jnp.int32)
        src = jnp.concatenate([_s, _d, _loop])
        dst = jnp.concatenate([_d, _s, _loop])
        _o = jnp.argsort(dst, stable=True)
        src = src[_o]
        dst = dst[_o]
        edge_weight = jax.random.uniform(jax.random.fold_in(_gk, 12), (41250,), jnp.float32, 0.0, 0.999999)
        return (x, src, dst, edge_weight)
    x, src, dst, edge_weight = _rec_inputs()

    def _L0_gnn_setup():
        import jax, jax.numpy as jnp
        import numpy as np
        N = 12500
        D_IN = 512
        D_OUT = 512
        E = 400000
        key = jax.random.key(seed)
        ks = jax.random.split(key, 10)
        stdv = 1.0 / np.sqrt(D_OUT)
        return {'x': jax.random.normal(ks[0], (N, D_IN), dtype=jnp.float32), 'w1': jax.random.uniform(ks[1], (D_IN, D_OUT), jnp.float32, -stdv, stdv), 'w2': jax.random.uniform(ks[2], (D_IN, D_OUT), jnp.float32, -stdv, stdv), 'w3': jax.random.uniform(ks[3], (D_IN, D_OUT), jnp.float32, -stdv, stdv), 'b1': jax.random.uniform(ks[4], (D_OUT,), jnp.float32, -stdv, stdv), 'b2': jax.random.uniform(ks[5], (D_OUT,), jnp.float32, -stdv, stdv), 'b3': jax.random.uniform(ks[6], (D_OUT,), jnp.float32, -stdv, stdv), 'edge_row': jax.random.randint(ks[7], (E,), 0, N, dtype=jnp.int32), 'edge_col': jax.random.randint(ks[8], (E,), 0, N, dtype=jnp.int32), 'edge_val': jax.random.uniform(ks[9], (E,), dtype=jnp.float32)}
    _L0_gnn_all = _L0_gnn_setup()
    _L0_gnn_in = {k: v for k, v in _L0_gnn_all.items() if k in ('w1', 'w2', 'w3', 'b1', 'b2', 'b3')}
    del _L0_gnn_all

    def _L0_ffn_setup():
        import jax, jax.numpy as jnp
        import numpy as np
        D_MODEL = 512
        D_FF = 256
        NUM_EXPERTS = 8
        TOP_K = 2
        key = jax.random.key(seed)
        ks = jax.random.split(key, 7)
        B, S = (4, 256)
        x = jax.random.normal(ks[0], (B, S, D_MODEL), dtype=jnp.float32)
        Wg = jax.random.normal(ks[1], (D_MODEL, NUM_EXPERTS), dtype=jnp.float32) * (1.0 / np.sqrt(D_MODEL))
        bg = jnp.zeros((NUM_EXPERTS,), dtype=jnp.float32)
        W1 = jax.random.normal(ks[2], (NUM_EXPERTS, D_MODEL, D_FF), dtype=jnp.float32) * (1.0 / np.sqrt(D_MODEL))
        b1 = jnp.zeros((NUM_EXPERTS, D_FF), dtype=jnp.float32)
        W2 = jax.random.normal(ks[3], (NUM_EXPERTS, D_FF, D_MODEL), dtype=jnp.float32) * (1.0 / np.sqrt(D_FF))
        b2 = jnp.zeros((NUM_EXPERTS, D_MODEL), dtype=jnp.float32)
        return {'x': x, 'Wg': Wg, 'bg': bg, 'W1': W1, 'b1': b1, 'W2': W2, 'b2': b2}
    _L0_ffn_all = _L0_ffn_setup()
    _L0_ffn_in = {k: v for k, v in _L0_ffn_all.items() if k in ('Wg', 'bg', 'W1', 'b1', 'W2', 'b2')}
    del _L0_ffn_all
    return {'x': x, 'src': src, 'dst': dst, 'edge_weight': edge_weight, 'L0_gnn_w1': _L0_gnn_in['w1'], 'L0_gnn_w2': _L0_gnn_in['w2'], 'L0_gnn_w3': _L0_gnn_in['w3'], 'L0_gnn_b1': _L0_gnn_in['b1'], 'L0_gnn_b2': _L0_gnn_in['b2'], 'L0_gnn_b3': _L0_gnn_in['b3'], 'L0_ffn_Wg': _L0_ffn_in['Wg'], 'L0_ffn_bg': _L0_ffn_in['bg'], 'L0_ffn_W1': _L0_ffn_in['W1'], 'L0_ffn_b1': _L0_ffn_in['b1'], 'L0_ffn_W2': _L0_ffn_in['W2'], 'L0_ffn_b2': _L0_ffn_in['b2']}

def reference(x, src, dst, edge_weight, L0_gnn_w1, L0_gnn_w2, L0_gnn_w3, L0_gnn_b1, L0_gnn_b2, L0_gnn_b3, L0_ffn_Wg, L0_ffn_bg, L0_ffn_W1, L0_ffn_b1, L0_ffn_W2, L0_ffn_b2):
    import jax
    import jax.numpy as jnp

    def _L0_gnn_ref(x, w1, w2, w3, b1, b2, b3, edge_row, edge_col, edge_val):
        import jax, jax.numpy as jnp
        import numpy as np
        N = 12500
        D_IN = 512
        D_OUT = 512
        E = 400000
        n = x.shape[0]
        support = x @ w1
        trans = x @ w2 + b2
        gate = jax.nn.sigmoid(x @ w3 + b3)
        msgs = support[edge_col] * edge_val[:, None]
        agg = jax.ops.segment_sum(msgs, edge_row, num_segments=n)
        out = jax.nn.relu(agg + b1)
        return trans + gate * (out - trans)

    def _L0_ffn_ref(x, Wg, bg, W1, b1, W2, b2):
        import jax, jax.numpy as jnp
        import numpy as np
        D_MODEL = 512
        D_FF = 256
        NUM_EXPERTS = 8
        TOP_K = 2
        B, S, D = x.shape
        x_flat = x.reshape(-1, D)
        gate_logits = x_flat @ Wg + bg
        gate_logits = gate_logits - jnp.max(gate_logits, axis=-1, keepdims=True)
        gate_top_k, gate_idx = jax.lax.top_k(gate_logits, TOP_K)
        gate_scores = jax.nn.softmax(gate_top_k, axis=-1)
        h = jax.nn.gelu(jnp.einsum('td,edf->etf', x_flat, W1) + b1[:, None, :], approximate=False)
        expert_out = jnp.einsum('etf,efd->etd', h, W2) + b2[:, None, :]
        expert_out = jnp.transpose(expert_out, (1, 0, 2))
        topk_out = jnp.take_along_axis(expert_out, gate_idx[:, :, None], axis=1)
        moe_out = jnp.sum(topk_out * gate_scores[:, :, None], axis=1)
        return moe_out.reshape(B, S, D) + x
    x = x + _L0_gnn_ref(_layernorm(x, axis=-1), L0_gnn_w1, L0_gnn_w2, L0_gnn_w3, L0_gnn_b1, L0_gnn_b2, L0_gnn_b3, src, dst, edge_weight)
    x = x + _L0_ffn_ref(_layernorm(x, axis=-1)[None], L0_ffn_Wg, L0_ffn_bg, L0_ffn_W1, L0_ffn_b1, L0_ffn_W2, L0_ffn_b2)[0]
    return x

_drawn_inputs = setup_inputs


def setup_inputs(seed=0):
    import zlib

    import numpy as np

    out = dict(_drawn_inputs(seed))
    spreads = {'L0_ffn_bg': (0.0, 0.1), 'L0_ffn_b1': (0.0, 0.364), 'L0_ffn_b2': (0.0, 0.1)}
    factors = {'L0_gnn_b1': 4.282, 'L0_gnn_b2': 3.503, 'L0_gnn_b3': 4.45}
    for name, (base, spread) in spreads.items():
        noise = np.random.default_rng([zlib.crc32(name.encode()), seed]).standard_normal(out[name].shape)
        drawn = base * np.exp(spread * noise) if base else spread * noise
        out[name] = jnp.asarray(drawn.astype(out[name].dtype))
    for name, factor in factors.items():
        out[name] = (out[name] * factor).astype(out[name].dtype)
    return out
```

```python
from contextlib import ExitStack

import concourse.bass as bass
from concourse import mybir

ALU = mybir.AluOpType
ACT = mybir.ActivationFunctionType
F32 = mybir.dt.float32
I32 = mybir.dt.int32
U32 = mybir.dt.uint32
DVE = mybir.EngineType.DVE
PE = mybir.EngineType.PE

P = 128
GROUP = 3
WINDOW = 16
EPS = 1e-5
TOP_K = 2


def split_shapes(n_nodes, n_edges):
    tiles = -(-n_nodes // P)
    tiles += tiles % 2
    pairs = tiles // 2
    groups = -(-n_edges // (P * GROUP))
    per_pair = -(-groups // pairs)
    per_pair += per_pair % 2
    return tiles, pairs, per_pair, per_pair * pairs


def gnn_moe_layer(nc, x, src, dst, first_dst, edge_w, w_gnn, b_gnn, wg, bg, w1, b1, w2, b2, out):
    D = x.shape[1]
    KD = D // P
    E, _, F = w1.shape
    KF = F // P
    T = x.shape[0] // P
    PAIRS = T // 2
    TOK = T * P
    NB = T
    GROUPS = first_dst.shape[1]
    EDGE_TILES = GROUPS * GROUP
    PER_PAIR = GROUPS // PAIRS
    COLS = NB * WINDOW
    WINDOWS = TOK // WINDOW
    BLOCK = 2 * P
    BLOCKS = TOK // BLOCK
    UNITS = 2 * BLOCKS
    assert D == 512 and COLS <= 512 and T % 2 == 0 and PER_PAIR % 2 == 0 and BLOCKS == PAIRS

    ctx = ExitStack()
    with ctx:

        def sb(name, shape, dt=F32):
            return ctx.enter_context(nc.sbuf_tensor(name, shape, dt))

        def ps(name, shape):
            return ctx.enter_context(nc.psum_tensor(name, shape, F32))

        def sem(name):
            return ctx.enter_context(nc.semaphore(name))

        ident = sb("ident", [P, P])
        iota = sb("iota", [P, COLS])
        ones_col = sb("ones_col", [P, 1])
        xs = sb("xs", [P, T, D])
        gate = sb("gate", [P, T, D])
        support = sb("support", [P, T, D])
        adj = sb("adj", [P, NB, TOK + WINDOW])
        adj_block = sb("adj_block", [P, TOK])
        adjT = sb("adjT", [P, 2, NB, P])
        wproj = sb("wproj", [P, 3 * KD * D])
        w_gnn_sb = wproj[:, :].rearrange("p (m k n) -> p m k n", m=3, k=KD)
        yT = wproj[:, 0:KD * TOK].rearrange("p (k n) -> p k n", k=KD)
        b_gnn_sb = sb("b_gnn_sb", [P, 3, D])
        xn = sb("xn", [P, 2, D])
        xT = sb("xT", [P, 2, KD, P])
        pair = sb("pair", [P, 2, D])
        trans, keep = pair[:, 0, :], pair[:, 1, :]
        x1 = pair
        mv2 = sb("mv2", [P, 2, 2])
        std2 = sb("std2", [P, 2])
        norm2 = sb("norm2", [P, 2, 2])
        stats = sb("stats", [P, T, 6])
        mv = sb("mv", [P, T, 2])
        std = sb("std", [P, T])
        norm = sb("norm", [P, T, 2])
        src_i = sb("src_i", [P, EDGE_TILES], I32)
        dst_i = sb("dst_i", [P, EDGE_TILES], I32)
        base_i = sb("base_i", [P, GROUPS], I32)
        edge_w_sb = sb("edge_w_sb", [P, EDGE_TILES])
        src_lo = src_i[:, :].bitcast(F32)
        dst_f = dst_i[:, :].bitcast(F32)
        block_i = sb("block_i", [P, EDGE_TILES], I32)
        block_col = block_i[:, :].bitcast(F32)
        outside = sb("outside", [P, EDGE_TILES])
        below = sb("below", [P, EDGE_TILES])
        col = sb("col", [P, EDGE_TILES])
        strays = sb("strays", [P, 1])
        strays_i = sb("strays_i", [1, 1], I32)
        now = sb("now", [P, 3, PER_PAIR * GROUP])
        rows = sb("rows", [P, 2, GROUP, P])
        cols = sb("cols", [P, 2, GROUP, COLS])
        wg_sb = sb("wg_sb", [P, KD, E])
        bg_sb = sb("bg_sb", [P, E])
        b1_sb = sb("b1_sb", [P, KF, E])
        b2_sb = sb("b2_sb", [E, D])
        w1_sb = sb("w1_sb", [P, 2, KD, F])
        w2_sb = sb("w2_sb", [P, 2, KF, D])
        hT = gate[:, 0:4, :].rearrange("p a d -> p (a d)")[:, 0:2 * KF * BLOCK].rearrange(
            "p (u f n) -> p u f n", u=2, f=KF)
        logits = sb("logits", [P, T, E])
        best = sb("best", [P, T, 8])
        best_i = sb("best_i", [P, T, 8], U32)
        best_f = sb("best_f", [P, T, 8])
        odds = sb("odds", [P, T])
        score = sb("score", [P, TOP_K, T])
        hit = sb("hit", [P, TOP_K, T, E])
        scores = sb("scores", [P, T, E])
        scores_now = sb("scores_now", [P, 2, T])
        scoresT = support[0:E, 0:3, :].rearrange("p a d -> p (a d)")[:, 0:TOK]

        bank = [ps(f"bank{i}", [P, 512]) for i in range(8)]
        turn_bank = bank[0:2]
        proj_bank = bank[2:5]
        edge_bank = bank[5:7]
        misc_bank = bank[7]
        agg_bank = bank[2:4]
        adj_bank = bank[4:7]
        up_bank = [[bank[0], bank[1]], [bank[4], bank[5]]]
        scoresT_bank = bank[6:8]
        down_bank = [bank[2], bank[3], bank[6], bank[7]]

        s_x = sem("s_x")
        s_edges = sem("s_edges")
        s_wproj = sem("s_wproj")
        s_small = sem("s_small")
        s_expert = [sem("s_expert_even"), sem("s_expert_odd")]
        s_zero = sem("s_zero")
        s_const = sem("s_const")
        s_adj_zero = sem("s_adj_zero")
        s_chain = sem("s_chain")
        s_var = sem("s_var")
        s_std = sem("s_std")
        s_norm = sem("s_norm")
        s_xn = sem("s_xn")
        s_turn = sem("s_turn")
        s_xT = sem("s_xT")
        s_proj = sem("s_proj")
        s_bank_free = [sem(f"s_bank{m}_free") for m in range(3)]
        s_support = sem("s_support")
        s_trans = sem("s_trans")
        s_trans_free = sem("s_trans_free")
        s_gate_in = sem("s_gate_in")
        s_gate = sem("s_gate")
        s_mix = sem("s_mix")
        s_onehot = sem("s_onehot")
        s_group = sem("s_group")
        s_flush = sem("s_flush")
        s_strays = sem("s_strays")
        s_count = sem("s_count")
        s_branch = sem("s_branch")
        s_redo = sem("s_redo")
        s_redo_onehot = sem("s_redo_onehot")
        s_redo_group = sem("s_redo_group")
        s_redo_flush = sem("s_redo_flush")
        s_now = sem("s_now")
        s_redo_copy = sem("s_redo_copy")
        s_rec2 = sem("s_rec2")
        s_adj_block = sem("s_adj_block")
        s_adj_turn = sem("s_adj_turn")
        s_adjT = sem("s_adjT")
        s_agg = sem("s_agg")
        s_relu = sem("s_relu")
        s_agg_free = sem("s_agg_free")
        s_x1 = sem("s_x1")
        s_ln = sem("s_ln")
        s_var2 = sem("s_var2")
        s_std2 = sem("s_std2")
        s_norm2 = sem("s_norm2")
        s_y = sem("s_y")
        s_turn2 = sem("s_turn2")
        s_yT = sem("s_yT")
        s_yT_kept = sem("s_yT_kept")
        s_x1y = sem("s_x1y")
        s_logits = sem("s_logits")
        s_logits_sb = sem("s_logits_sb")
        s_gap = sem("s_gap")
        s_odds = sem("s_odds")
        s_scores = sem("s_scores")
        s_scoresT = sem("s_scoresT")
        s_scoresT_sb = sem("s_scoresT_sb")
        s_scores_now = sem("s_scores_now")
        s_bias = sem("s_bias")
        s_up = sem("s_up")
        s_h = sem("s_h")
        s_down = sem("s_down")
        s_down_free = sem("s_down_free")
        s_out = sem("s_out")
        s_settled = sem("s_settled")

        block = ctx.enter_context(nc.Block())

        def tile(a, t):
            return a[:, bass.ds(t, 1), :].rearrange("p a d -> p (a d)")

        def one(a, t, j):
            return a[:, bass.ds(t, 1), j]

        def settle(eng):
            eng.sem_inc(s_settled, 1)

        @block.sync
        def _(sp):
            sp.dma_start(dst_i[:, :], dst).then_inc(s_edges, 16)
            sp.dma_start(base_i[:, :], first_dst.broadcast_to([P, GROUPS])).then_inc(s_edges, 16)
            sp.dma_start(src_i[:, :], src).then_inc(s_edges, 16)
            sp.dma_start(edge_w_sb[:, :], edge_w).then_inc(s_edges, 16)
            sp.dma_start(xs[:, :, :], x.rearrange("(t p) d -> p t d", p=P)).then_inc(s_x, 16)
            for m in range(3):
                sp.dma_start(w_gnn_sb[:, m, :, :], w_gnn[m].rearrange("(k p) n -> p k n", p=P)).then_inc(s_wproj, 16)
            for m in range(3):
                sp.dma_start(b_gnn_sb[:, m, :], b_gnn[m:m + 1, :].broadcast_to([P, D])).then_inc(s_small, 16)
            sp.dma_start(wg_sb[:, :, :], wg.rearrange("(k p) e -> p k e", p=P)).then_inc(s_small, 16)
            sp.dma_start(bg_sb[:, :], bg.broadcast_to([P, E])).then_inc(s_small, 16)
            sp.dma_start(b1_sb[:, :, :], b1).then_inc(s_small, 16)
            sp.dma_start(b2_sb[:, :], b2).then_inc(s_small, 16)

            def load_expert(e, u):
                sp.dma_start(w1_sb[:, u, :, :],
                             w1[bass.ds(e, 1)].rearrange("a (k p) f -> p (a k) f", p=P)).then_inc(s_expert[u], 16)
                sp.dma_start(w2_sb[:, u, :, :],
                             w2[bass.ds(e, 1)].rearrange("a (k p) n -> p (a k) n", p=P)).then_inc(s_expert[u], 16)

            load_expert(0, 0)
            load_expert(1, 1)
            with sp.Fori(0, E // 2 - 1) as i:
                for u in range(2):
                    sp.wait_ge(s_down, i * 2 * T + (u + 1) * T)
                    load_expert(i * 2 + u + 2, u)
            for t in range(T):
                sp.wait_ge(s_down_free, 4 + T + (E - 1) * T + t + 1)
                sp.dma_start(out[t * P:(t + 1) * P, :], xs[:, t, :]).then_inc(s_out, 16)
            sp.wait_ge(s_out, 16 * T)

        @block.gpsimd
        def _(pool):
            pool.memset(ident[:, :], 0.0).then_inc(s_zero, 1)
            pool.iota(iota[:, :], [[1, COLS]], base=0, channel_multiplier=0,
                      allow_small_or_imprecise_dtypes=True).then_inc(s_const, 1)
            pool.memset(ones_col[:, :], 1.0).then_inc(s_const, 1)
            pool.wait_ge(s_zero, 1)
            pool.affine_select(out=ident[:, :], in_=ident[:, :], compare_op=ALU.not_equal, fill=1.0,
                               base=0, pattern=[[-1, P]], channel_multiplier=1).then_inc(s_const, 1)
            pool.memset(adj[:, :, :], 0.0).then_inc(s_adj_zero, 1)

            with pool.Fori(0, PAIRS) as i:
                for u in range(2):
                    t = i * 2 + u
                    xt, gt = tile(xs, t), tile(gate, t)
                    pool.wait_ge(s_trans, t + 1)
                    pool.wait_ge(s_gate, t + 1)
                    pool.tensor_tensor(keep, trans, gt, ALU.mult).then_inc(s_mix, 1)
                    pool.wait_ge(s_mix, t * 2 + 1)
                    pool.tensor_tensor(keep, trans, keep, ALU.subtract).then_inc(s_mix, 1)
                    pool.wait_ge(s_mix, t * 2 + 2)
                    pool.tensor_tensor(xt, xt, keep, ALU.add).then_inc(s_trans_free, 1)

            with pool.Fori(0, PAIRS) as i:
                for u in range(2):
                    t = i * 2 + u
                    xt = tile(xs, t)
                    pool.wait_ge(s_y, t + 1)
                    pool.tensor_tensor(xt, x1[:, u, :], xn[:, u, :], ALU.add).then_inc(s_x1y, 1)
                    pool.wait_ge(s_yT, t + 1)
                    pool.tensor_copy(yT[:, :, bass.ds(t * P, P)], xT[:, u, :, :]).then_inc(s_yT_kept, 1)

        @block.scalar
        def _(act):
            act.sem_inc(s_bank_free[0], 1)

            def normalize(t, u):
                act.activation(xn[:, u, :], tile(xs, t), ACT.Identity,
                               bias=one(norm, t, 1), scale=one(norm, t, 0)).then_inc(s_xn, 1)

            def turned(u, done):
                act.activation(xT[:, u, :, :], turn_bank[u][:, :].rearrange("p (k n) -> p k n", k=KD),
                               ACT.Copy).then_inc(done, 1)

            act.wait_ge(s_var, 1)
            act.activation(std[:, :], mv[:, :, 1], ACT.Sqrt).then_inc(s_std, 1)
            act.wait_ge(s_norm, 1)
            act.preload_act_table(ACT.Sigmoid)
            normalize(0, 0)
            normalize(1, 1)
            act.wait_ge(s_turn, 1)
            turned(0, s_xT)

            def project_pair(i, last):
                for u in range(2):
                    t = i * 2 + u
                    act.wait_ge(s_proj, t * 3 + 1)
                    settle(act)
                    act.activation(tile(support, t), proj_bank[0][:, :], ACT.Copy).then_inc(s_support, 1)
                    act.wait_ge(s_support, t + 1)
                    act.sem_inc(s_bank_free[0], 1)
                    if not (last and u):
                        act.wait_ge(s_turn, t + 2)
                        turned(1 - u, s_xT)
                    act.wait_ge(s_gate_in, t + 1)
                    settle(act)
                    act.activation(tile(gate, t), tile(gate, t), ACT.Sigmoid).then_inc(s_gate, 1)
                    if not last:
                        normalize(t + 2, u)

            with act.Fori(0, PAIRS - 1) as i:
                project_pair(i, False)
            project_pair(PAIRS - 1, True)

            act.preload_act_table(ACT.Sqrt)
            def turned_adj(t, u):
                act.wait_ge(s_adj_turn, t + 1)
                for c in range(3):
                    n = min(4, NB - 4 * c)
                    ins = act.activation(adjT[:, u, 4 * c:4 * c + n, :],
                                         adj_bank[c][:, 0:n * P].rearrange("p (k n) -> p k n", n=P), ACT.Copy)
                ins.then_inc(s_adjT, 1)

            def normalize_pair(i, last):
                for u in range(2):
                    t = i * 2 + u
                    if not last:
                        turned_adj(t + 2, u)
                    act.wait_ge(s_var2, t + 1)
                    act.activation(std2[:, u:u + 1], mv2[:, u, 1:2], ACT.Sqrt).then_inc(s_std2, 1)
                    act.wait_ge(s_norm2, t + 1)
                    act.wait_ge(s_x1y, t + 1)
                    act.activation(xn[:, u, :], x1[:, u, :], ACT.Identity,
                                   bias=norm2[:, u, 1:2], scale=norm2[:, u, 0:1]).then_inc(s_y, 1)
                    act.wait_ge(s_turn2, t + 1)
                    act.wait_ge(s_yT_kept, t + 1)
                    turned(u, s_yT)
                    act.wait_ge(s_logits, t + 1)
                    settle(act)
                    act.activation(tile(logits, t), misc_bank[:, 256 + u * E:256 + (u + 1) * E],
                                   ACT.Copy).then_inc(s_logits_sb, 1)

            turned_adj(0, 0)
            turned_adj(1, 1)
            with act.Fori(0, PAIRS - 1) as i:
                normalize_pair(i, False)
            normalize_pair(PAIRS - 1, True)

            act.wait_ge(s_gap, 1)
            act.activation(odds[:, :], odds[:, :], ACT.Exp).then_inc(s_odds, 1)
            for t in range(T):
                act.wait_ge(s_scoresT, t + 1)
                act.activation(scoresT[:, t * P:(t + 1) * P], scoresT_bank[t % 2][0:E, 0:P],
                               ACT.Copy).then_inc(s_scoresT_sb, 1)

            act.preload_act_table(ACT.Gelu)
            with act.Fori(0, E // 2) as i:
                for n in range(UNITS):
                    act.wait_ge(s_up, i * UNITS + n + 1)
                    settle(act)
                    for f in range(KF):
                        ins = act.activation(hT[:, n % 2, f, :], up_bank[n % 2][f][:, 0:BLOCK], ACT.Gelu,
                                             bias=b1_sb[:, f, bass.ds(i * 2 + n // BLOCKS, 1)])
                    ins.then_inc(s_h, 1)

        @block.tensor
        def _(pe):
            def turn(u, done):
                for k in range(KD):
                    ins = pe.transpose(turn_bank[u][:, k * P:(k + 1) * P], xn[:, u, k * P:(k + 1) * P], ident[:, :])
                ins.then_inc(done, 1)

            def edge_products(bank, slot, done):
                for j in range(GROUP):
                    ins = pe.matmul(bank[:, 0:COLS], rows[:, slot, j, :], cols[:, slot, j, :],
                                    start=(j == 0), stop=(j == GROUP - 1))
                ins.then_inc(done, 1)

            pe.wait_ge(s_const, 3)
            pe.wait_ge(s_xn, 1)
            turn(0, s_turn)
            pe.wait_ge(s_wproj, 16 * 3)

            def project_pair(i, last):
                g = 0
                for u in range(2):
                    t = i * 2 + u
                    for m in range(3):
                        for k in range(KD):
                            if g < PER_PAIR:
                                pe.wait_ge(s_onehot, i * PER_PAIR + g + 1)
                                edge_products(edge_bank[g % 2], g % 2, s_group)
                                g += 1
                            if k == 0:
                                if m == 0:
                                    pe.wait_ge(s_xT, t + 1)
                                pe.wait_ge(s_bank_free[m], t + 1)
                            ins = pe.matmul(proj_bank[m][:, :], xT[:, u, k, :], w_gnn_sb[:, m, k, :],
                                            start=(k == 0), stop=(k == KD - 1))
                        ins.then_inc(s_proj, 1)
                        if m == 1 and not (last and u):
                            pe.wait_ge(s_xn, t + 2)
                            turn(1 - u, s_turn)

            with pe.Fori(0, PAIRS - 1) as i:
                project_pair(i, False)
            project_pair(PAIRS - 1, True)

            pe.wait_ge(s_strays, 1)
            pe.matmul(misc_bank[0:1, 0:1], strays[:, :], ones_col[:, :], start=True, stop=True).then_inc(s_count, 1)
            pe.wait_ge(s_branch, 1)
            found = nc.values_load(strays_i[0:1, 0:1], engines=[PE], min_val=0, max_val=1)
            with pe.If(found == 0):
                pe.nop()
            with pe.Else():
                with pe.Fori(0, WINDOWS) as w:
                    with pe.Fori(0, GROUPS) as g:
                        pe.wait_ge(s_redo_onehot, w * GROUPS + g + 1)
                        edge_products(edge_bank[0], 0, s_redo_group)

            def turn_adj(t):
                pe.wait_ge(s_adj_block, t + 1)
                for k in range(NB):
                    ins = pe.transpose(adj_bank[k // 4][:, (k % 4) * P:(k % 4 + 1) * P],
                                       adj_block[:, k * P:(k + 1) * P], ident[:, :])
                ins.then_inc(s_adj_turn, 1)

            def aggregate(t, u):
                pe.wait_ge(s_adjT, t + 1)
                pe.wait_ge(s_agg_free, t + 1)
                for k in range(NB):
                    ins = pe.matmul(agg_bank[u][:, :], adjT[:, u, k, :], support[:, k, :],
                                    start=(k == 0), stop=(k == NB - 1))
                ins.then_inc(s_agg, 1)

            def turn_y(t, u):
                pe.wait_ge(s_y, t + 1)
                turn(u, s_turn2)
                pe.wait_ge(s_yT, t + 1)
                for k in range(KD):
                    ins = pe.matmul(misc_bank[:, 256 + u * E:256 + (u + 1) * E], xT[:, u, k, :], wg_sb[:, k, :],
                                    start=(k == 0), stop=(k == KD - 1))
                ins.then_inc(s_logits, 1)

            pe.wait_ge(s_support, T)
            pe.wait_ge(s_small, 16 * 7)
            turn_adj(0)
            pe.wait_ge(s_adjT, 1)
            turn_adj(1)
            aggregate(0, 0)
            with pe.Fori(0, PAIRS - 1) as i:
                for u in range(2):
                    aggregate(i * 2 + u + 1, 1 - u)
                    turn_adj(i * 2 + u + 2)
                    turn_y(i * 2 + u, u)
            aggregate(T - 1, 1)
            turn_y(T - 2, 0)
            turn_y(T - 1, 1)

            pe.wait_ge(s_scores, 1)
            for t in range(T):
                if t >= 2:
                    pe.wait_ge(s_scoresT_sb, t - 1)
                pe.transpose(scoresT_bank[t % 2][0:E, 0:P], scores[:, t, :],
                             ident[:, :]).then_inc(s_scoresT, 1)
            pe.wait_ge(s_scoresT_sb, T)
            for t in range(T):
                pe.wait_ge(s_down_free, t + 1)
                pe.matmul(down_bank[t % 4][:, :], scoresT[:, t * P:(t + 1) * P], b2_sb[:, :],
                          start=True, stop=True).then_inc(s_bias, 1)

            def up(i, n):
                e, c = n // BLOCKS, n % BLOCKS
                if c == 0:
                    pe.wait_ge(s_expert[e], i * 32 + 32)
                for f in range(KF):
                    for k in range(KD):
                        ins = pe.matmul(up_bank[n % 2][f][:, 0:BLOCK], w1_sb[:, e, k, f * P:(f + 1) * P],
                                        yT[:, k, c * BLOCK:(c + 1) * BLOCK], start=(k == 0), stop=(k == KD - 1))
                ins.then_inc(s_up, 1)

            def down(i, n):
                e = n // BLOCKS
                pe.wait_ge(s_h, i * UNITS + n + 1)
                for v in range(2):
                    o = T + 2 * n + v
                    pe.wait_ge(s_down_free, i * (2 * UNITS) + o + 1)
                    for f in range(KF):
                        ins = pe.matmul(down_bank[o % 4][:, :], hT[:, n % 2, f, v * P:(v + 1) * P],
                                        w2_sb[:, e, f, :], start=(f == 0), stop=(f == KF - 1))
                    ins.then_inc(s_down, 1)

            pe.wait_ge(s_yT_kept, T + 2)
            with pe.Fori(0, E // 2) as i:
                up(i, 0)
                for n in range(UNITS):
                    if n + 1 < UNITS:
                        up(i, n + 1)
                    down(i, n)

        @block.vector
        def _(dve):
            dve.sem_inc(s_bank_free[1], 1)
            dve.sem_inc(s_bank_free[2], 1)
            dve.sem_inc(s_trans_free, 1)
            dve.sem_inc(s_agg_free, 2)
            dve.sem_inc(s_x1y, 2)
            dve.sem_inc(s_yT_kept, 2)
            dve.sem_inc(s_down_free, 4)

            chained = [0]

            def link(ins):
                chained[0] += 1
                ins.then_inc(s_chain, 1)
                dve.wait_ge(s_chain, chained[0])

            dve.wait_ge(s_edges, 64)
            dve.tensor_scalar(block_i[:, :], src_i[:, :], 7, None, ALU.logical_shift_right)
            dve.tensor_copy(dst_f, dst_i[:, :])
            link(dve.tensor_copy(below[:, 0:GROUPS], base_i[:, :]))
            dve.tensor_scalar(src_i[:, :], src_i[:, :], P - 1, None, ALU.bitwise_and)
            link(dve.tensor_tensor(col[:, :].rearrange("p (g j) -> p g j", j=GROUP),
                                   dst_f.rearrange("p (g j) -> p g j", j=GROUP),
                                   below[:, 0:GROUPS].unsqueeze(2).broadcast_to([P, GROUPS, GROUP]),
                                   ALU.subtract))
            dve.tensor_copy(src_lo, src_i[:, :])
            link(dve.tensor_scalar(block_col, block_i[:, :], float(WINDOW), None, ALU.mult))

            def columns():
                link(dve.tensor_scalar(outside[:, :], col[:, :], float(WINDOW), None, ALU.is_ge))
                link(dve.tensor_scalar(below[:, :], col[:, :], 0.0, None, ALU.is_lt))
                link(dve.tensor_tensor(outside[:, :], outside[:, :], below[:, :], ALU.add))

            columns()
            link(dve.tensor_tensor(col[:, :], col[:, :], block_col, ALU.add))
            dve.tensor_reduce(strays[:, :], outside[:, :], mybir.AxisListType.X, ALU.max).then_inc(s_strays, 1)
            link(dve.scalar_tensor_tensor(col[:, :], outside[:, :], float(2 * TOK), col[:, :], ALU.mult, ALU.add))

            dve.wait_ge(s_x, 16)
            for t in range(T):
                ins = dve.bn_stats(stats[:, t, :], xs[:, t, :])
            link(ins)
            for t in range(T):
                ins = dve.bn_aggr(mv[:, t, :], stats[:, t, :])
            link(ins)
            dve.tensor_scalar(mv[:, :, 1], mv[:, :, 1], EPS, None, ALU.add).then_inc(s_var, 1)
            dve.wait_ge(s_std, 1)
            link(dve.reciprocal(norm[:, :, 0], std[:, :]))
            dve.scalar_tensor_tensor(norm[:, :, 1], mv[:, :, 0], -1.0, norm[:, :, 0],
                                     ALU.mult, ALU.mult).then_inc(s_norm, 1)

            def onehots(slot, picked, first, done):
                for j in range(GROUP):
                    c = first + j
                    dve.tensor_scalar(rows[:, slot, j, :], iota[:, 0:P], picked[:, 0, c:c + 1],
                                      picked[:, 1, c:c + 1], ALU.is_equal, ALU.mult)
                    ins = dve.tensor_scalar(cols[:, slot, j, :], iota[:, :], picked[:, 2, c:c + 1],
                                            None, ALU.is_equal)
                ins.then_inc(done, 1)

            def add_to_adj(bank, first, done):
                window = adj[:, :, bass.ds(first, WINDOW)]
                dve.tensor_tensor(window, bank[:, 0:COLS].rearrange("p (b w) -> p b w", w=WINDOW), window,
                                  ALU.add).then_inc(done, 1)

            dve.wait_ge(s_const, 3)
            dve.wait_ge(s_adj_zero, 1)
            dve.sem_inc(s_flush, 1)

            def pair_of_tiles(i):
                for a, edges in enumerate((src_lo, edge_w_sb[:, :], col[:, :])):
                    ins = dve.tensor_copy(now[:, a, :], edges[:, bass.ds(i * (PER_PAIR * GROUP), PER_PAIR * GROUP)])
                ins.then_inc(s_now, 1)
                dve.wait_ge(s_now, i + 1)

                def flush(g):
                    n = i * PER_PAIR + g
                    dve.wait_ge(s_group, n + 1)
                    dve.wait_ge(s_flush, n + 1)
                    first = nc.values_load(base_i[0:1, bass.ds(n, 1)], engines=[DVE], min_val=0, max_val=TOK,
                                           skip_runtime_bounds_check_because="destinations are nodes")
                    add_to_adj(edge_bank[g % 2], first, s_flush)

                def take_trans(u):
                    t = i * 2 + u
                    dve.wait_ge(s_proj, t * 3 + 2)
                    dve.wait_ge(s_trans_free, t + 1)
                    dve.tensor_tensor(trans, proj_bank[1][:, :], b_gnn_sb[:, 1, :], ALU.add).then_inc(s_trans, 1)
                    dve.wait_ge(s_trans, t + 1)
                    dve.sem_inc(s_bank_free[1], 1)

                def take_gate(u):
                    t = i * 2 + u
                    dve.wait_ge(s_proj, t * 3 + 3)
                    dve.tensor_tensor(tile(gate, t), proj_bank[2][:, :], b_gnn_sb[:, 2, :],
                                      ALU.add).then_inc(s_gate_in, 1)
                    dve.wait_ge(s_gate_in, t + 1)
                    dve.sem_inc(s_bank_free[2], 1)

                for g in range(PER_PAIR):
                    if g >= 2:
                        flush(g - 2)
                    onehots(g % 2, now, g * GROUP, s_onehot)
                    if g == 9:
                        take_trans(0)
                    if g == 13:
                        take_gate(0)
                take_trans(1)
                flush(PER_PAIR - 2)
                flush(PER_PAIR - 1)
                take_gate(1)

            dve.wait_ge(s_small, 16 * 7)
            with dve.Fori(0, PAIRS) as i:
                pair_of_tiles(i)

            dve.wait_ge(s_count, 1)
            dve.tensor_scalar(strays_i[:, :], misc_bank[0:1, 0:1], 1.0, None, ALU.min).then_inc(s_branch, 1)
            dve.wait_ge(s_branch, 1)
            found = nc.values_load(strays_i[0:1, 0:1], engines=[DVE], min_val=0, max_val=1)
            with dve.If(found == 0):
                dve.nop()
            with dve.Else():
                dve.memset(adj[:, :, :], 0.0).then_inc(s_redo, 1)
                dve.wait_ge(s_redo, 1)
                with dve.Fori(0, WINDOWS) as w:
                    dve.tensor_copy(col[:, :], dst_f).then_inc(s_redo, 1)
                    dve.wait_ge(s_redo, w * 6 + 2)
                    dve.tensor_scalar(outside[:, :], col[:, :], float(WINDOW), None, ALU.is_ge)
                    dve.tensor_scalar(below[:, :], col[:, :], 0.0, None, ALU.is_lt).then_inc(s_redo, 1)
                    dve.wait_ge(s_redo, w * 6 + 3)
                    dve.tensor_tensor(outside[:, :], outside[:, :], below[:, :], ALU.add).then_inc(s_redo, 1)
                    dve.wait_ge(s_redo, w * 6 + 4)
                    dve.tensor_tensor(col[:, :], col[:, :], block_col, ALU.add).then_inc(s_redo, 1)
                    dve.wait_ge(s_redo, w * 6 + 5)
                    dve.scalar_tensor_tensor(col[:, :], outside[:, :], float(2 * TOK), col[:, :],
                                             ALU.mult, ALU.add)
                    dve.tensor_scalar(dst_f, dst_f, -float(WINDOW), None, ALU.add).then_inc(s_redo, 2)
                    dve.wait_ge(s_redo, w * 6 + 7)
                    settle(dve)
                    with dve.Fori(0, GROUPS) as g:
                        n = w * GROUPS + g
                        for a, edges in enumerate((src_lo, edge_w_sb[:, :], col[:, :])):
                            ins = dve.tensor_copy(now[:, a, 0:GROUP], edges[:, bass.ds(g * GROUP, GROUP)])
                        ins.then_inc(s_redo_copy, 1)
                        dve.wait_ge(s_redo_copy, n + 1)
                        onehots(0, now, 0, s_redo_onehot)
                        dve.wait_ge(s_redo_group, n + 1)
                        add_to_adj(edge_bank[0], w * WINDOW, s_redo_flush)
                        dve.wait_ge(s_redo_flush, n + 1)

            def stage(t):
                dve.tensor_copy(adj_block[:, :], adj[:, bass.ds(t, 1), 0:TOK].rearrange("p a n -> p (a n)")
                                ).then_inc(s_adj_block, 1)

            dve.wait_ge(s_flush, GROUPS + 1)
            dve.wait_ge(s_trans_free, T + 1)
            stage(0)
            dve.wait_ge(s_adj_turn, 1)
            stage(1)

            def finish_pair(i, last):
                for u in range(2):
                    t = i * 2 + u
                    xt, gt = tile(xs, t), tile(gate, t)
                    x1t = x1[:, u, :]
                    dve.wait_ge(s_agg, t + 1)
                    dve.wait_ge(s_x1y, t + 1)
                    dve.tensor_tensor(x1t, agg_bank[u][:, :], b_gnn_sb[:, 0, :], ALU.add).then_inc(s_agg_free, 1)
                    if not last:
                        dve.wait_ge(s_adj_turn, t + 2)
                        settle(dve)
                        stage(t + 2)
                    dve.wait_ge(s_agg_free, t + 3)
                    dve.scalar_tensor_tensor(x1t, x1t, 0.0, gt, ALU.max, ALU.mult).then_inc(s_relu, 1)
                    dve.wait_ge(s_relu, t + 1)
                    dve.tensor_tensor(x1t, xt, x1t, ALU.add).then_inc(s_x1, 1)
                    dve.wait_ge(s_x1, t + 1)
                    dve.bn_stats(stats[:, u, :], x1t).then_inc(s_ln, 1)
                    dve.wait_ge(s_ln, t * 2 + 1)
                    settle(dve)
                    dve.bn_aggr(mv2[:, u, :], stats[:, u, :]).then_inc(s_ln, 1)
                    dve.wait_ge(s_ln, t * 2 + 2)
                    dve.tensor_scalar(mv2[:, u, 1:2], mv2[:, u, 1:2], EPS, None, ALU.add).then_inc(s_var2, 1)
                    dve.wait_ge(s_std2, t + 1)
                    dve.reciprocal(norm2[:, u, 0:1], std2[:, u:u + 1]).then_inc(s_rec2, 1)
                    dve.wait_ge(s_rec2, t + 1)
                    dve.scalar_tensor_tensor(norm2[:, u, 1:2], mv2[:, u, 0:1], -1.0, norm2[:, u, 0:1],
                                             ALU.mult, ALU.mult).then_inc(s_norm2, 1)

            with dve.Fori(0, PAIRS - 1) as i:
                finish_pair(i, False)
            finish_pair(PAIRS - 1, True)

            dve.wait_ge(s_logits_sb, T)
            link(dve.tensor_tensor(logits[:, :, :], logits[:, :, :],
                                   bg_sb[:, :].unsqueeze(1).broadcast_to([P, T, E]), ALU.add))
            for t in range(T):
                ins = dve.max(best[:, t, :], logits[:, t, :])
            link(ins)
            dve.tensor_tensor(odds[:, :], best[:, :, 1], best[:, :, 0], ALU.subtract).then_inc(s_gap, 1)
            for t in range(T):
                ins = dve.max_index(best_i[:, t, :], best[:, t, :], logits[:, t, :])
            link(ins)
            link(dve.tensor_copy(best_f[:, :, :], best_i[:, :, :]))
            for j in range(TOP_K):
                ins = dve.tensor_tensor(hit[:, j, :, :], iota[:, 0:E].unsqueeze(1).broadcast_to([P, T, E]),
                                        best_f[:, :, j:j + 1].broadcast_to([P, T, E]), ALU.is_equal)
            dve.wait_ge(s_odds, 1)
            link(dve.tensor_scalar(score[:, 1, :], odds[:, :], 1.0, None, ALU.add))
            link(dve.reciprocal(score[:, 0, :], score[:, 1, :]))
            link(dve.tensor_tensor(score[:, 1, :], score[:, 0, :], odds[:, :], ALU.mult))
            for j in range(TOP_K):
                ins = dve.tensor_tensor(hit[:, j, :, :], hit[:, j, :, :],
                                        score[:, j, :].unsqueeze(2).broadcast_to([P, T, E]), ALU.mult)
            link(ins)
            dve.tensor_tensor(scores[:, :, :], hit[:, 0, :, :], hit[:, 1, :, :], ALU.add).then_inc(s_scores, 1)

            dve.wait_ge(s_x1y, T + 2)
            for t in range(T):
                dve.wait_ge(s_bias, t + 1)
                dve.tensor_tensor(xs[:, t, :], down_bank[t % 4][:, :], xs[:, t, :], ALU.add).then_inc(s_down_free, 1)
            dve.wait_ge(s_scores, 1)
            with dve.Fori(0, E // 2) as i:
                dve.wait_ge(s_down_free, i * (2 * UNITS) + 4 + T)
                for e in range(2):
                    ins = dve.tensor_copy(scores_now[:, e, :], scores[:, :, bass.ds(i * 2 + e, 1)].rearrange("p t a -> p (t a)"))
                ins.then_inc(s_scores_now, 1)
                dve.wait_ge(s_scores_now, i + 1)
                for n in range(UNITS):
                    for v in range(2):
                        o = 2 * n + v
                        t = o % T
                        dve.wait_ge(s_down, i * (2 * UNITS) + o + 1)
                        dve.scalar_tensor_tensor(xs[:, t, :], down_bank[(T + o) % 4][:, :],
                                                 scores_now[:, n // BLOCKS, t:t + 1], xs[:, t, :],
                                                 ALU.mult, ALU.add).then_inc(s_down_free, 1)


def kernel(x, src, dst, edge_weight, L0_gnn_w1, L0_gnn_w2, L0_gnn_w3, L0_gnn_b1, L0_gnn_b2, L0_gnn_b3,
           L0_ffn_Wg, L0_ffn_bg, L0_ffn_W1, L0_ffn_b1, L0_ffn_W2, L0_ffn_b2):
    import numpy as np
    from concourse import bacc
    from concourse.bass_utils import run_bass_kernel_spmd

    x, src, dst, edge_weight = (np.asarray(a) for a in (x, src, dst, edge_weight))
    n, d = x.shape
    tiles, pairs, per_pair, groups = split_shapes(n, len(src))
    slots = groups * GROUP * P
    more = slots - len(src)

    def by_tile(a):
        return np.ascontiguousarray(a.reshape(groups * GROUP, P).T)

    src_p = np.pad(src, (0, more), mode="edge")
    dst_p = np.pad(dst, (0, more), mode="edge")
    e, _, f = np.shape(L0_ffn_W1)
    arrays = {
        "x": np.pad(x, ((0, tiles * P - n), (0, 0))),
        "src": by_tile(src_p),
        "dst": by_tile(dst_p),
        "first_dst": np.ascontiguousarray(dst_p[:: GROUP * P][None, :]),
        "edge_w": by_tile(np.pad(edge_weight, (0, more))),
        "w_gnn": np.stack([L0_gnn_w1, L0_gnn_w2, L0_gnn_w3]),
        "b_gnn": np.stack([L0_gnn_b1, L0_gnn_b2, L0_gnn_b3]),
        "wg": np.asarray(L0_ffn_Wg),
        "bg": np.asarray(L0_ffn_bg)[None, :],
        "w1": np.asarray(L0_ffn_W1),
        "b1": np.ascontiguousarray(np.asarray(L0_ffn_b1).reshape(e, f // P, P).transpose(2, 1, 0)),
        "w2": np.asarray(L0_ffn_W2),
        "b2": np.asarray(L0_ffn_b2),
    }
    nc = bacc.Bacc("TRN2", target_bir_lowering=False, num_devices=1)
    args = {
        name: nc.dram_tensor(f"in_{name}", a.shape, mybir.dt.from_np(a.dtype), kind="ExternalInput").ap()
        for name, a in arrays.items()
    }
    out = nc.dram_tensor("out", (tiles * P, d), F32, kind="ExternalOutput").ap()
    gnn_moe_layer(nc, out=out, **args)
    r = run_bass_kernel_spmd(nc, [{f"in_{name}": a for name, a in arrays.items()}], core_ids=[0])
    return r.results[0]["out"][:n]
```

```python
from contextlib import ExitStack

import numpy as np

import concourse.bass as bass
from concourse import mybir

ALU = mybir.AluOpType
ACT = mybir.ActivationFunctionType
F32 = mybir.dt.float32
I32 = mybir.dt.int32
U32 = mybir.dt.uint32
DVE = mybir.EngineType.DVE
PE = mybir.EngineType.PE

P = 128
GROUP = 3
WINDOW = 16
EPS = 1e-5
TOP_K = 2
CAP_TILES = 3


def split_shapes(n_nodes, n_edges):
    tiles = -(-n_nodes // P)
    tiles += tiles % 2
    pairs = tiles // 2
    groups = -(-n_edges // (P * GROUP))
    per_pair = -(-groups // pairs)
    per_pair += per_pair % 2
    return tiles, pairs, per_pair, per_pair * pairs


def gnn_moe_layer(nc, x, src, dst, first_dst, edge_w, w_gnn, b_gnn, wg, bg, w1, b1, w2, b2, out, y_rows, routes, n_nodes):
    D = x.shape[1]
    KD = D // P
    E, _, F = w1.shape
    KF = F // P
    T = x.shape[0] // P
    PAIRS = T // 2
    TOK = T * P
    NB = T
    GROUPS = first_dst.shape[1]
    EDGE_TILES = GROUPS * GROUP
    PER_PAIR = GROUPS // PAIRS
    COLS = NB * WINDOW
    WINDOWS = TOK // WINDOW
    ROUTES = E * T
    CAP = CAP_TILES * P
    assert D == 512 and COLS <= 512 and T % 2 == 0 and T >= 6 and PER_PAIR % 2 == 0 and E <= 8

    ctx = ExitStack()
    with ctx:

        def sb(name, shape, dt=F32):
            return ctx.enter_context(nc.sbuf_tensor(name, shape, dt))

        def ps(name, shape):
            return ctx.enter_context(nc.psum_tensor(name, shape, F32))

        def sem(name):
            return ctx.enter_context(nc.semaphore(name))

        ident = sb("ident", [P, P])
        iota = sb("iota", [P, COLS])
        ones = sb("ones", [P, P])
        ones_col = ones[:, 0:1]
        before = sb("before", [P, P])
        real = sb("real", [P, 1])
        unreal_row = sb("unreal_row", [P, TOP_K])
        token_i = sb("token_i", [P, T], I32)
        xs = sb("xs", [P, T, D])
        gate = sb("gate", [P, T, D])
        support = sb("support", [P, T, D])
        adj = sb("adj", [P, NB, TOK + WINDOW])
        adj_block = sb("adj_block", [P, TOK])
        adjT = sb("adjT", [P, 2, NB, P])
        wproj = sb("wproj", [P, 3 * KD * D])
        w_gnn_sb = wproj[:, :].rearrange("p (m k n) -> p m k n", m=3, k=KD)
        b2_sb = wproj[:, 0:E * D].rearrange("p (e d) -> p e d", e=E)
        b_gnn_sb = sb("b_gnn_sb", [P, 3, D])
        xn = sb("xn", [P, 2, D])
        xT = sb("xT", [P, 2, KD, P])
        pair = sb("pair", [P, 2, D])
        trans, keep = pair[:, 0, :], pair[:, 1, :]
        x1 = pair
        mv2 = sb("mv2", [P, 2, 2])
        std2 = sb("std2", [P, 2])
        norm2 = sb("norm2", [P, 2, 2])
        stats = sb("stats", [P, T, 6])
        mv = sb("mv", [P, T, 2])
        std = sb("std", [P, T])
        norm = sb("norm", [P, T, 2])
        src_i = sb("src_i", [P, EDGE_TILES], I32)
        dst_i = sb("dst_i", [P, EDGE_TILES], I32)
        base_i = sb("base_i", [P, GROUPS], I32)
        edge_w_sb = sb("edge_w_sb", [P, EDGE_TILES])
        src_lo = src_i[:, :].bitcast(F32)
        dst_f = dst_i[:, :].bitcast(F32)
        block_i = sb("block_i", [P, EDGE_TILES], I32)
        block_col = block_i[:, :].bitcast(F32)
        outside = sb("outside", [P, EDGE_TILES])
        below = sb("below", [P, EDGE_TILES])
        col = sb("col", [P, EDGE_TILES])
        strays = sb("strays", [P, 1])
        strays_i = sb("strays_i", [1, 1], I32)
        now = sb("now", [P, 3, PER_PAIR * GROUP])
        rows = sb("rows", [P, 2, GROUP, P])
        cols = sb("cols", [P, 2, GROUP, COLS])
        wg_sb = sb("wg_sb", [P, KD, E])
        bg_sb = sb("bg_sb", [P, E])
        b1_sb = sb("b1_sb", [P, KF, E])
        w1_sb = sb("w1_sb", [P, 2, KD, F])
        w2_sb = sb("w2_sb", [P, 2, KF, D])
        logits = sb("logits", [P, 2, E])
        best = sb("best", [P, 2, 8])
        best_i = sb("best_i", [P, 2, 8], U32)
        best_f = sb("best_f", [P, 2, TOP_K])
        odds = sb("odds", [P, 2])
        odds1 = sb("odds1", [P, 2])
        hit = sb("hit", [P, 2, TOP_K, E])
        chosen = sb("chosen", [P, 2, E])
        chosen_sum = sb("chosen_sum", [P, 2, E])
        hit_rank = sb("hit_rank", [P, 2, TOP_K, E])
        rank = sb("rank", [P, 2, TOP_K])
        rank_i = sb("rank_i", [P, 2, TOP_K], I32)
        rank_tile_i = sb("rank_tile_i", [P, 2, TOP_K], I32)
        rank_tile = sb("rank_tile", [P, 2, TOP_K])
        first_col = sb("first_col", [P, 2, TOP_K])
        row = sb("row", [P, 2, TOP_K])
        row_i = sb("row_i", [P, 2, TOP_K, 1], I32)
        route = sb("route", [P, 2, TOP_K, 2], I32)
        route_score = route[:, :, :, :].rearrange("p u j a -> p (u j a)").bitcast(F32).rearrange(
            "p (u j a) -> p u j a", u=2, a=2)
        table = sb("table", [P, ROUTES, 2], I32)
        table_score = table[:, :, :].rearrange("p r a -> p (r a)").bitcast(F32).rearrange("p (r a) -> p r a", a=2)
        most = sb("most", [1, 1])
        over_i = sb("over_i", [1, 1], I32)
        get_token = sb("get_token", [P, 2, CAP_TILES], I32)
        put_token = sb("put_token", [P, 2, CAP_TILES], I32)

        room = adj[:, :, :].rearrange("p b n -> p (b n)")
        taken = 0

        def carve(*shape):
            nonlocal taken
            size = int(np.prod(shape))
            a = room[:, taken:taken + size]
            taken += size
            return a

        y_in = carve(2, CAP_TILES, D).rearrange("p (u c d) -> p u c d", u=2, c=CAP_TILES)
        y_inT = carve(KD, CAP).rearrange("p (k n) -> p k n", k=KD)
        hT = carve(KF, CAP).rearrange("p (f n) -> p f n", f=KF)
        y_out = carve(2, CAP_TILES, D).rearrange("p (u c d) -> p u c d", u=2, c=CAP_TILES)

        bank = [ps(f"bank{i}", [P, 512]) for i in range(8)]
        turn_bank = bank[0:2]
        proj_bank = bank[2:5]
        edge_bank = bank[5:7]
        misc_bank = bank[7]
        agg_bank = bank[2:4]
        adj_bank = bank[4:7]
        in_bank = [bank[0], bank[1], bank[7]]
        up_bank = bank[2:4]
        down_bank = bank[4:7]

        s_x = sem("s_x")
        s_edges = sem("s_edges")
        s_wproj = sem("s_wproj")
        s_small = sem("s_small")
        s_expert = [sem("s_expert_even"), sem("s_expert_odd")]
        s_zero = sem("s_zero")
        s_const = sem("s_const")
        s_adj_zero = sem("s_adj_zero")
        s_chain = sem("s_chain")
        s_var = sem("s_var")
        s_std = sem("s_std")
        s_norm = sem("s_norm")
        s_xn = sem("s_xn")
        s_turn = sem("s_turn")
        s_xT = sem("s_xT")
        s_proj = sem("s_proj")
        s_bank_free = [sem(f"s_bank{m}_free") for m in range(3)]
        s_support = sem("s_support")
        s_trans = sem("s_trans")
        s_trans_free = sem("s_trans_free")
        s_gate_in = sem("s_gate_in")
        s_gate = sem("s_gate")
        s_mix = sem("s_mix")
        s_onehot = sem("s_onehot")
        s_group = sem("s_group")
        s_flush = sem("s_flush")
        s_strays = sem("s_strays")
        s_count = sem("s_count")
        s_branch = sem("s_branch")
        s_redo = sem("s_redo")
        s_redo_onehot = sem("s_redo_onehot")
        s_redo_group = sem("s_redo_group")
        s_redo_flush = sem("s_redo_flush")
        s_now = sem("s_now")
        s_redo_copy = sem("s_redo_copy")
        s_rec2 = sem("s_rec2")
        s_adj_block = sem("s_adj_block")
        s_adj_turn = sem("s_adj_turn")
        s_adjT = sem("s_adjT")
        s_agg = sem("s_agg")
        s_relu = sem("s_relu")
        s_agg_free = sem("s_agg_free")
        s_x1 = sem("s_x1")
        s_ln = sem("s_ln")
        s_var2 = sem("s_var2")
        s_std2 = sem("s_std2")
        s_norm2 = sem("s_norm2")
        s_y = sem("s_y")
        s_turn2 = sem("s_turn2")
        s_yT = sem("s_yT")
        s_x1y = sem("s_x1y")
        s_y_saved = [sem("s_y_saved_even"), sem("s_y_saved_odd")]
        s_out = sem("s_out")
        s_zeros = sem("s_zeros")
        s_ahead = sem("s_ahead")
        s_filled = sem("s_filled")
        s_b2 = sem("s_b2")
        s_logits = sem("s_logits")
        s_pick = sem("s_pick")
        s_gap = sem("s_gap")
        s_odds = sem("s_odds")
        s_chosen = sem("s_chosen")
        s_rank = sem("s_rank")
        s_placing = sem("s_placing")
        s_place = sem("s_place")
        s_routed = sem("s_routed")
        s_route_saved = [sem("s_route_saved_even"), sem("s_route_saved_odd")]
        s_table = sem("s_table")
        s_counts = sem("s_counts")
        s_over = sem("s_over")
        s_get_token = sem("s_get_token")
        s_got = [sem("s_got_even"), sem("s_got_odd")]
        s_in_turned = sem("s_in_turned")
        s_y_inT = sem("s_y_inT")
        s_up = sem("s_up")
        s_h = sem("s_h")
        s_down = sem("s_down")
        s_taken = sem("s_taken")
        s_scaled = sem("s_scaled")
        s_put_token = sem("s_put_token")
        s_y_out_free = sem("s_y_out_free")
        s_added = [sem("s_added_even"), sem("s_added_odd")]
        s_more_expert = sem("s_more_expert")
        s_more_token = sem("s_more_token")
        s_more_got = sem("s_more_got")
        s_more_turned = sem("s_more_turned")
        s_more_inT = sem("s_more_inT")
        s_more_up = sem("s_more_up")
        s_more_h = sem("s_more_h")
        s_more_down = sem("s_more_down")
        s_more_taken = sem("s_more_taken")
        s_more_scaled = sem("s_more_scaled")
        s_more_added = sem("s_more_added")
        s_settled = sem("s_settled")

        block = ctx.enter_context(nc.Block())

        def tile(a, t):
            return a[:, bass.ds(t, 1), :].rearrange("p a d -> p (a d)")

        def one(a, t, j):
            return a[:, bass.ds(t, 1), j]

        def settle(eng):
            eng.sem_inc(s_settled, 1)

        MORE = T - CAP_TILES

        def beyond_share(eng, kind, body):
            eng.wait_ge(s_over, 1)
            over = nc.values_load(over_i[0:1, 0:1], engines=[kind], min_val=0, max_val=1)
            with eng.If(over == 0):
                eng.nop()
            with eng.Else():
                body()

        @block.sync
        def _(sp):
            sp.dma_start(dst_i[:, :], dst).then_inc(s_edges, 16)
            sp.dma_start(base_i[:, :], first_dst.broadcast_to([P, GROUPS])).then_inc(s_edges, 16)
            sp.dma_start(src_i[:, :], src).then_inc(s_edges, 16)
            sp.dma_start(edge_w_sb[:, :], edge_w).then_inc(s_edges, 16)
            sp.dma_start(xs[:, :, :], x.rearrange("(t p) d -> p t d", p=P)).then_inc(s_x, 16)
            for m in range(3):
                sp.dma_start(w_gnn_sb[:, m, :, :], w_gnn[m].rearrange("(k p) n -> p k n", p=P)).then_inc(s_wproj, 16)
            for m in range(3):
                sp.dma_start(b_gnn_sb[:, m, :], b_gnn[m:m + 1, :].broadcast_to([P, D])).then_inc(s_small, 16)
            sp.dma_start(wg_sb[:, :, :], wg.rearrange("(k p) e -> p k e", p=P)).then_inc(s_small, 16)
            sp.dma_start(bg_sb[:, :], bg.broadcast_to([P, E])).then_inc(s_small, 16)
            sp.dma_start(b1_sb[:, :, :], b1).then_inc(s_small, 16)

            def load_expert(e, u):
                sp.dma_start(w1_sb[:, u, :, :],
                             w1[bass.ds(e, 1)].rearrange("a (k p) f -> p (a k) f", p=P)).then_inc(s_expert[u], 16)
                sp.dma_start(w2_sb[:, u, :, :],
                             w2[bass.ds(e, 1)].rearrange("a (k p) n -> p (a k) n", p=P)).then_inc(s_expert[u], 16)

            sp.wait_ge(s_zeros, 1)
            for rows_out in (y_rows, out):
                sp.dma_start(rows_out[TOK:TOK + CAP, :].rearrange("(c p) d -> p c d", p=P),
                             gate[:, 0:CAP_TILES, :]).then_inc(s_filled, 16)
            sp.wait_ge(s_ahead, 1)
            sp.dma_start(routes[0:P * ROUTES, :].rearrange("(p r) a -> p (r a)", p=P),
                         table[:, :, :].rearrange("p r a -> p (r a)")).then_inc(s_filled, 16)
            load_expert(0, 0)
            load_expert(1, 1)
            sp.wait_ge(s_proj, 3 * T)
            sp.dma_start(b2_sb, b2.broadcast_to([P, E * D])).then_inc(s_b2, 16)
            with sp.Fori(0, PAIRS) as i:
                for u in range(2):
                    t = i * 2 + u
                    sp.wait_ge(s_y, t + 1)
                    sp.dma_start(y_rows[bass.ds(t * P, P), :], xn[:, u, :]).then_inc(s_y_saved[u], 16)
                    sp.wait_ge(s_x1y, t + 3)
                    sp.dma_start(out[bass.ds(t * P, P), :], tile(xs, t)).then_inc(s_out, 16)
            for u in range(2):
                sp.wait_ge(s_route_saved[u], 16 * TOP_K * PAIRS)
            sp.dma_start(table[:, :, :].rearrange("p r a -> p (r a)"),
                         routes[0:P * ROUTES, :].rearrange("(p r) a -> p (r a)", p=P)).then_inc(s_table, 16)
            with sp.Fori(0, E // 2 - 1) as i:
                for u in range(2):
                    e = i * 2 + u
                    sp.wait_ge(s_down, e * CAP_TILES + CAP_TILES)
                    load_expert(e + 2, u)

            def load_more():
                sp.wait_ge(s_down, E * CAP_TILES)
                with sp.Fori(0, E) as e:
                    sp.wait_ge(s_more_down, e * MORE + 1)
                    sp.dma_start(w1_sb[:, 0, :, :],
                                 w1[bass.ds(e, 1)].rearrange("a (k p) f -> p (a k) f", p=P)).then_inc(s_more_expert, 16)
                    sp.dma_start(w2_sb[:, 0, :, :],
                                 w2[bass.ds(e, 1)].rearrange("a (k p) n -> p (a k) n", p=P)).then_inc(s_more_expert, 16)

            beyond_share(sp, mybir.EngineType.SP, load_more)
            for u in range(2):
                sp.wait_ge(s_added[u], 16 * CAP_TILES * (E // 2))

        @block.gpsimd
        def _(pool):
            pool.memset(ident[:, :], 0.0).then_inc(s_zero, 1)
            pool.iota(iota[:, :], [[1, COLS]], base=0, channel_multiplier=0,
                      allow_small_or_imprecise_dtypes=True).then_inc(s_const, 1)
            pool.memset(ones[:, :], 1.0).then_inc(s_const, 1)
            pool.wait_ge(s_zero, 1)
            pool.affine_select(out=ident[:, :], in_=ident[:, :], compare_op=ALU.not_equal, fill=1.0,
                               base=0, pattern=[[-1, P]], channel_multiplier=1).then_inc(s_const, 1)
            pool.memset(adj[:, :, :], 0.0).then_inc(s_adj_zero, 1)
            pool.memset(gate[:, 0:CAP_TILES, :], 0.0).then_inc(s_zeros, 1)
            pool.memset(table[:, :, :], 0).then_inc(s_zero, 1)
            pool.wait_ge(s_zero, 2)
            token_of = table[:, :, :].rearrange("p (e c) a -> p e c a", e=E)
            for c in range(CAP_TILES):
                last = T if c == CAP_TILES - 1 else c + 1
                ins = pool.iota(token_of[:, :, c:last, 0], [[0, E], [0, last - c]], base=TOK + c * P,
                                channel_multiplier=1)
                ins.then_inc(s_zero, 1)
            pool.wait_ge(s_zero, 2 + CAP_TILES)
            pool.iota(token_i[:, :], [[P, T]], base=0, channel_multiplier=1).then_inc(s_ahead, 1)
            nodes = n_nodes - (T - 1) * P
            pool.memset(real[:, :], 1.0).then_inc(s_zero, 1)
            pool.iota(unreal_row[:, :], [[1, TOP_K]], base=P * ROUTES, channel_multiplier=TOP_K,
                      allow_small_or_imprecise_dtypes=True).then_inc(s_zero, 1)
            pool.wait_ge(s_const, 3)
            pool.affine_select(out=before[:, :], in_=ones[:, :], compare_op=ALU.is_gt, fill=0.0,
                               base=0, pattern=[[1, P]], channel_multiplier=-1).then_inc(s_ahead, 1)
            pool.wait_ge(s_zero, 4 + CAP_TILES)
            pool.affine_select(out=real[:, :], in_=real[:, :], compare_op=ALU.is_gt, fill=0.0,
                               base=nodes, pattern=[[0, 1]], channel_multiplier=-1).then_inc(s_ahead, 1)
            pool.affine_select(out=unreal_row[:, :], in_=unreal_row[:, :], compare_op=ALU.is_ge, fill=0.0,
                               base=-nodes, pattern=[[0, TOP_K]], channel_multiplier=1).then_inc(s_ahead, 1)

            with pool.Fori(0, PAIRS) as i:
                for u in range(2):
                    t = i * 2 + u
                    xt, gt = tile(xs, t), tile(gate, t)
                    pool.wait_ge(s_trans, t + 1)
                    pool.wait_ge(s_gate, t + 1)
                    pool.tensor_tensor(keep, trans, gt, ALU.mult).then_inc(s_mix, 1)
                    pool.wait_ge(s_mix, t * 2 + 1)
                    pool.tensor_tensor(keep, trans, keep, ALU.subtract).then_inc(s_mix, 1)
                    pool.wait_ge(s_mix, t * 2 + 2)
                    pool.tensor_tensor(xt, xt, keep, ALU.add).then_inc(s_trans_free, 1)

            def add_y(t, u):
                pool.wait_ge(s_y, t + 1)
                pool.tensor_tensor(tile(xs, t), x1[:, u, :], xn[:, u, :], ALU.add).then_inc(s_x1y, 1)

            def save_routes(t, u):
                pool.wait_ge(s_routed, t + 1)
                settle(pool)
                for j in range(TOP_K):
                    pool.indirect_dma_start(routes[:, :], bass.IndirectOffsetOnAxis(ap=row_i[:, u, j, :], axis=0),
                                            route[:, u, j, :], None).then_inc(s_route_saved[u], 16)

            add_y(0, 0)
            add_y(1, 1)
            pool.wait_ge(s_filled, 16 * 3)
            with pool.Fori(1, PAIRS) as i:
                for u in range(2):
                    save_routes(i * 2 + u - 2, u)
                    add_y(i * 2 + u, u)
            save_routes(T - 2, 0)
            save_routes(T - 1, 1)

            def get(e, i, u):
                pool.tensor_copy(get_token[:, u, :], table[:, bass.ds(e * T, CAP_TILES), 0]).then_inc(s_get_token, 1)
                pool.wait_ge(s_get_token, e + 1)
                settle(pool)
                for c in range(CAP_TILES):
                    pool.indirect_dma_start(y_in[:, u, c, :], None, y_rows[:, :],
                                            bass.IndirectOffsetOnAxis(ap=get_token[:, u, c:c + 1], axis=0)
                                            ).then_inc(s_got[u], 16)

            def put(e, i, u, first=False):
                pool.tensor_copy(put_token[:, u, :], table[:, bass.ds(e * T, CAP_TILES), 0]).then_inc(s_put_token, 1)
                pool.wait_ge(s_put_token, e + 1)
                pool.wait_ge(s_scaled, e * CAP_TILES + CAP_TILES)
                if not first:
                    pool.wait_ge(s_added[1 - u], (i + u) * (16 * CAP_TILES))
                pool.sem_inc(s_y_out_free, 1)
                for c in range(CAP_TILES):
                    pool.indirect_dma_start(out[:, :], bass.IndirectOffsetOnAxis(ap=put_token[:, u, c:c + 1], axis=0),
                                            y_out[:, u, c, :], None, compute_op=ALU.add).then_inc(s_added[u], 16)

            for u in range(2):
                pool.wait_ge(s_y_saved[u], 16 * PAIRS)
            pool.wait_ge(s_table, 16)
            get(0, 0, 0)
            get(1, 0, 1)
            pool.wait_ge(s_out, 16 * T)

            def put_and_get(i, u, first):
                e = i * 2 + u
                pool.wait_ge(s_in_turned, e * CAP_TILES + CAP_TILES)
                get(e + 2, i + 1, u)
                put(e, i, u, first)

            put_and_get(0, 0, True)
            put_and_get(0, 1, False)
            with pool.Fori(1, E // 2 - 1) as i:
                put_and_get(i, 0, False)
                put_and_get(i, 1, False)
            put(E - 2, E // 2 - 1, 0)
            put(E - 1, E // 2 - 1, 1)

            def move_more():
                for u in range(2):
                    pool.wait_ge(s_added[u], 16 * CAP_TILES * (E // 2))
                pool.wait_ge(s_in_turned, E * CAP_TILES)
                with pool.Fori(0, E) as e:
                    with pool.Fori(0, MORE) as c:
                        n = e * MORE + c
                        pool.tensor_copy(get_token[:, 0, 0:1],
                                         table[:, bass.ds(e * T + c + CAP_TILES, 1), 0]).then_inc(s_more_token, 1)
                        pool.wait_ge(s_more_token, n + 1)
                        settle(pool)
                        pool.indirect_dma_start(y_in[:, 0, 0, :], None, y_rows[:, :],
                                                bass.IndirectOffsetOnAxis(ap=get_token[:, 0, 0:1], axis=0)
                                                ).then_inc(s_more_got, 16)
                        pool.wait_ge(s_more_scaled, n + 1)
                        settle(pool)
                        pool.indirect_dma_start(out[:, :],
                                                bass.IndirectOffsetOnAxis(ap=get_token[:, 0, 0:1], axis=0),
                                                y_out[:, 0, 0, :], None, compute_op=ALU.add).then_inc(s_more_added, 16)
                        pool.wait_ge(s_more_added, n * 16 + 16)

            beyond_share(pool, mybir.EngineType.Pool, move_more)

        @block.scalar
        def _(act):
            act.sem_inc(s_bank_free[0], 1)

            def normalize(t, u):
                act.activation(xn[:, u, :], tile(xs, t), ACT.Identity,
                               bias=one(norm, t, 1), scale=one(norm, t, 0)).then_inc(s_xn, 1)

            def turned(u, done):
                act.activation(xT[:, u, :, :], turn_bank[u][:, :].rearrange("p (k n) -> p k n", k=KD),
                               ACT.Copy).then_inc(done, 1)

            act.wait_ge(s_var, 1)
            act.activation(std[:, :], mv[:, :, 1], ACT.Sqrt).then_inc(s_std, 1)
            act.wait_ge(s_norm, 1)
            act.preload_act_table(ACT.Sigmoid)
            normalize(0, 0)
            normalize(1, 1)
            act.wait_ge(s_turn, 1)
            turned(0, s_xT)

            def project_pair(i, last):
                for u in range(2):
                    t = i * 2 + u
                    act.wait_ge(s_proj, t * 3 + 1)
                    settle(act)
                    act.activation(tile(support, t), proj_bank[0][:, :], ACT.Copy).then_inc(s_support, 1)
                    act.wait_ge(s_support, t + 1)
                    act.sem_inc(s_bank_free[0], 1)
                    if not (last and u):
                        act.wait_ge(s_turn, t + 2)
                        turned(1 - u, s_xT)
                    act.wait_ge(s_gate_in, t + 1)
                    settle(act)
                    act.activation(tile(gate, t), tile(gate, t), ACT.Sigmoid).then_inc(s_gate, 1)
                    if not last:
                        normalize(t + 2, u)

            with act.Fori(0, PAIRS - 1) as i:
                project_pair(i, False)
            project_pair(PAIRS - 1, True)

            act.preload_act_table(ACT.Sqrt)
            def turned_adj(t, u):
                act.wait_ge(s_adj_turn, t + 1)
                for c in range(3):
                    n = min(4, NB - 4 * c)
                    ins = act.activation(adjT[:, u, 4 * c:4 * c + n, :],
                                         adj_bank[c][:, 0:n * P].rearrange("p (k n) -> p k n", n=P), ACT.Copy)
                ins.then_inc(s_adjT, 1)

            def normalize_y(i, u, more, route):
                t = i * 2 + u
                act.wait_ge(s_var2, t + 1)
                act.activation(std2[:, u:u + 1], mv2[:, u, 1:2], ACT.Sqrt).then_inc(s_std2, 1)
                act.wait_ge(s_norm2, t + 1)
                act.wait_ge(s_x1y, t + 1)
                if route:
                    act.wait_ge(s_y_saved[u], i * 16)
                act.activation(xn[:, u, :], x1[:, u, :], ACT.Identity,
                               bias=norm2[:, u, 1:2], scale=norm2[:, u, 0:1]).then_inc(s_y, 1)
                if route:
                    exp_gap(t - 1, 1 - u)
                    act.preload_act_table(ACT.Sqrt)
                if more:
                    turned_adj(t + 2, u)
                act.wait_ge(s_turn2, t + 1)
                turned(u, s_yT)

            def exp_gap(t, u):
                act.wait_ge(s_gap, t + 1)
                act.activation(odds[:, u:u + 1], odds[:, u:u + 1], ACT.Exp).then_inc(s_odds, 1)

            turned_adj(0, 0)
            turned_adj(1, 1)
            normalize_y(0, 0, True, False)
            normalize_y(0, 1, True, False)
            exp_gap(0, 0)
            act.preload_act_table(ACT.Sqrt)
            with act.Fori(1, PAIRS - 1) as i:
                for u in range(2):
                    normalize_y(i, u, True, True)
            normalize_y(PAIRS - 1, 0, False, True)
            normalize_y(PAIRS - 1, 1, False, True)
            exp_gap(T - 1, 1)

            act.preload_act_table(ACT.Gelu)

            def turned_in(c, done):
                act.activation(y_inT[:, :, c * P:(c + 1) * P],
                               in_bank[c][:, :].rearrange("p (k n) -> p k n", k=KD), ACT.Copy).then_inc(done, 1)

            def gelu(e, n, done):
                for f in range(KF):
                    ins = act.activation(hT[:, f, 0:n], up_bank[f][:, 0:n], ACT.Gelu,
                                         bias=b1_sb[:, f, bass.ds(e, 1)])
                ins.then_inc(done, 1)

            with act.Fori(0, E) as e:
                for c in range(CAP_TILES):
                    act.wait_ge(s_in_turned, e * CAP_TILES + c + 1)
                    turned_in(c, s_y_inT)
                act.wait_ge(s_up, e + 1)
                settle(act)
                gelu(e, CAP, s_h)

            def gelu_more():
                with act.Fori(0, E) as e:
                    with act.Fori(0, MORE) as c:
                        n = e * MORE + c
                        act.wait_ge(s_more_turned, n + 1)
                        turned_in(0, s_more_inT)
                        act.wait_ge(s_more_up, n + 1)
                        settle(act)
                        gelu(e, P, s_more_h)

            beyond_share(act, mybir.EngineType.Activation, gelu_more)

        @block.tensor
        def _(pe):
            def turn(u, done):
                for k in range(KD):
                    ins = pe.transpose(turn_bank[u][:, k * P:(k + 1) * P], xn[:, u, k * P:(k + 1) * P], ident[:, :])
                ins.then_inc(done, 1)

            def edge_products(bank, slot, done):
                for j in range(GROUP):
                    ins = pe.matmul(bank[:, 0:COLS], rows[:, slot, j, :], cols[:, slot, j, :],
                                    start=(j == 0), stop=(j == GROUP - 1))
                ins.then_inc(done, 1)

            pe.wait_ge(s_const, 3)
            pe.wait_ge(s_xn, 1)
            turn(0, s_turn)
            pe.wait_ge(s_wproj, 16 * 3)

            def project_pair(i, last):
                g = 0
                for u in range(2):
                    t = i * 2 + u
                    for m in range(3):
                        for k in range(KD):
                            if g < PER_PAIR:
                                pe.wait_ge(s_onehot, i * PER_PAIR + g + 1)
                                edge_products(edge_bank[g % 2], g % 2, s_group)
                                g += 1
                            if k == 0:
                                if m == 0:
                                    pe.wait_ge(s_xT, t + 1)
                                pe.wait_ge(s_bank_free[m], t + 1)
                            ins = pe.matmul(proj_bank[m][:, :], xT[:, u, k, :], w_gnn_sb[:, m, k, :],
                                            start=(k == 0), stop=(k == KD - 1))
                        ins.then_inc(s_proj, 1)
                        if m == 1 and not (last and u):
                            pe.wait_ge(s_xn, t + 2)
                            turn(1 - u, s_turn)

            with pe.Fori(0, PAIRS - 1) as i:
                project_pair(i, False)
            project_pair(PAIRS - 1, True)

            pe.wait_ge(s_strays, 1)
            pe.matmul(misc_bank[0:1, 0:1], strays[:, :], ones_col[:, :], start=True, stop=True).then_inc(s_count, 1)
            pe.wait_ge(s_branch, 1)
            found = nc.values_load(strays_i[0:1, 0:1], engines=[PE], min_val=0, max_val=1)
            with pe.If(found == 0):
                pe.nop()
            with pe.Else():
                with pe.Fori(0, WINDOWS) as w:
                    with pe.Fori(0, GROUPS) as g:
                        pe.wait_ge(s_redo_onehot, w * GROUPS + g + 1)
                        edge_products(edge_bank[0], 0, s_redo_group)

            def turn_adj(t):
                pe.wait_ge(s_adj_block, t + 1)
                for k in range(NB):
                    ins = pe.transpose(adj_bank[k // 4][:, (k % 4) * P:(k % 4 + 1) * P],
                                       adj_block[:, k * P:(k + 1) * P], ident[:, :])
                ins.then_inc(s_adj_turn, 1)

            def aggregate(t, u):
                pe.wait_ge(s_adjT, t + 1)
                pe.wait_ge(s_agg_free, t + 1)
                for k in range(NB):
                    ins = pe.matmul(agg_bank[u][:, :], adjT[:, u, k, :], support[:, k, :],
                                    start=(k == 0), stop=(k == NB - 1))
                ins.then_inc(s_agg, 1)

            def turn_y(t, u, placed):
                pe.wait_ge(s_y, t + 1)
                turn(u, s_turn2)
                pe.wait_ge(s_yT, t + 1)
                if placed:
                    pe.wait_ge(s_placing, t)
                for k in range(KD):
                    ins = pe.matmul(misc_bank[:, 256 + u * E:256 + (u + 1) * E], xT[:, u, k, :], wg_sb[:, k, :],
                                    start=(k == 0), stop=(k == KD - 1))
                ins.then_inc(s_logits, 1)

            def rank_tile_of(t, u, first):
                pe.wait_ge(s_chosen, t + 1)
                ins = pe.matmul(misc_bank[:, 320:320 + E], before[:, :], chosen[:, u, :], start=True, stop=first)
                if not first:
                    ins = pe.matmul(misc_bank[:, 320:320 + E], ones[:, :], chosen_sum[:, 1 - u, :],
                                    start=False, stop=True)
                ins.then_inc(s_rank, 1)

            pe.wait_ge(s_support, T)
            pe.wait_ge(s_small, 16 * 6)
            turn_adj(0)
            pe.wait_ge(s_adjT, 1)
            turn_adj(1)
            aggregate(0, 0)
            aggregate(1, 1)
            turn_adj(2)
            turn_y(0, 0, False)
            aggregate(2, 0)
            pe.wait_ge(s_ahead, 4)
            rank_tile_of(0, 0, True)
            turn_adj(3)
            turn_y(1, 1, True)
            with pe.Fori(1, PAIRS - 1) as i:
                for u in range(2):
                    t = i * 2 + u
                    aggregate(t + 1, 1 - u)
                    rank_tile_of(t - 1, 1 - u, False)
                    turn_adj(t + 2)
                    turn_y(t, u, True)
            aggregate(T - 1, 1)
            rank_tile_of(T - 3, 1, False)
            turn_y(T - 2, 0, True)
            rank_tile_of(T - 2, 0, False)
            turn_y(T - 1, 1, True)
            rank_tile_of(T - 1, 1, False)
            pe.wait_ge(s_placing, T)
            pe.matmul(misc_bank[:, 384:384 + E], ones[:, :], chosen_sum[:, 1, :], start=True, stop=True
                      ).then_inc(s_counts, 1)
            pe.wait_ge(s_over, 1)

            def turn_in(e, i, u):
                pe.wait_ge(s_got[u], i * (16 * CAP_TILES) + 16 * CAP_TILES)
                for c in range(CAP_TILES):
                    turn_rows(y_in[:, u, c, :], in_bank[c], s_in_turned)

            def turn_rows(y_tile, to, done):
                for k in range(KD):
                    ins = pe.transpose(to[:, k * P:(k + 1) * P], y_tile[:, k * P:(k + 1) * P], ident[:, :])
                ins.then_inc(done, 1)

            def up(u, n, done):
                for f in range(KF):
                    for k in range(KD):
                        ins = pe.matmul(up_bank[f][:, 0:n], w1_sb[:, u, k, f * P:(f + 1) * P],
                                        y_inT[:, k, 0:n], start=(k == 0), stop=(k == KD - 1))
                ins.then_inc(done, 1)

            def down(u, c, done):
                for f in range(KF):
                    ins = pe.matmul(down_bank[c][:, :], hT[:, f, c * P:(c + 1) * P], w2_sb[:, u, f, :],
                                    start=(f == 0), stop=(f == KF - 1))
                ins.then_inc(done, 1)

            def expert(i, u, last):
                e = i * 2 + u
                pe.wait_ge(s_expert[u], i * 32 + 32)
                pe.wait_ge(s_y_inT, e * CAP_TILES + CAP_TILES)
                up(u, CAP, s_up)
                if not last:
                    turn_in(e + 1, i + u, 1 - u)
                pe.wait_ge(s_h, e + 1)
                for c in range(CAP_TILES):
                    pe.wait_ge(s_taken, e * CAP_TILES + c + 1)
                    down(u, c, s_down)

            turn_in(0, 0, 0)
            with pe.Fori(0, E // 2 - 1) as i:
                expert(i, 0, False)
                expert(i, 1, False)
            expert(E // 2 - 1, 0, False)
            expert(E // 2 - 1, 1, True)

            def multiply_more():
                with pe.Fori(0, E) as e:
                    pe.wait_ge(s_more_expert, e * 32 + 32)
                    settle(pe)
                    with pe.Fori(0, MORE) as c:
                        n = e * MORE + c
                        pe.wait_ge(s_more_got, n * 16 + 16)
                        turn_rows(y_in[:, 0, 0, :], in_bank[0], s_more_turned)
                        pe.wait_ge(s_more_inT, n + 1)
                        up(0, P, s_more_up)
                        pe.wait_ge(s_more_h, n + 1)
                        pe.wait_ge(s_more_taken, n + 1)
                        down(0, 0, s_more_down)

            pe.wait_ge(s_taken, E * CAP_TILES + CAP_TILES)
            beyond_share(pe, PE, multiply_more)

        @block.vector
        def _(dve):
            dve.sem_inc(s_bank_free[1], 1)
            dve.sem_inc(s_bank_free[2], 1)
            dve.sem_inc(s_trans_free, 1)
            dve.sem_inc(s_agg_free, 2)
            dve.sem_inc(s_x1y, 2)
            dve.sem_inc(s_taken, CAP_TILES)
            dve.sem_inc(s_more_taken, 1)
            dve.sem_inc(s_more_down, 1)
            dve.sem_inc(s_y_out_free, 1)

            chained = [0]

            def link(ins):
                chained[0] += 1
                ins.then_inc(s_chain, 1)
                dve.wait_ge(s_chain, chained[0])

            dve.wait_ge(s_edges, 64)
            dve.tensor_scalar(block_i[:, :], src_i[:, :], 7, None, ALU.logical_shift_right)
            dve.tensor_copy(dst_f, dst_i[:, :])
            link(dve.tensor_copy(below[:, 0:GROUPS], base_i[:, :]))
            dve.tensor_scalar(src_i[:, :], src_i[:, :], P - 1, None, ALU.bitwise_and)
            link(dve.tensor_tensor(col[:, :].rearrange("p (g j) -> p g j", j=GROUP),
                                   dst_f.rearrange("p (g j) -> p g j", j=GROUP),
                                   below[:, 0:GROUPS].unsqueeze(2).broadcast_to([P, GROUPS, GROUP]),
                                   ALU.subtract))
            dve.tensor_copy(src_lo, src_i[:, :])
            link(dve.tensor_scalar(block_col, block_i[:, :], float(WINDOW), None, ALU.mult))

            def columns():
                link(dve.tensor_scalar(outside[:, :], col[:, :], float(WINDOW), None, ALU.is_ge))
                link(dve.tensor_scalar(below[:, :], col[:, :], 0.0, None, ALU.is_lt))
                link(dve.tensor_tensor(outside[:, :], outside[:, :], below[:, :], ALU.add))

            columns()
            link(dve.tensor_tensor(col[:, :], col[:, :], block_col, ALU.add))
            dve.tensor_reduce(strays[:, :], outside[:, :], mybir.AxisListType.X, ALU.max).then_inc(s_strays, 1)
            link(dve.scalar_tensor_tensor(col[:, :], outside[:, :], float(2 * TOK), col[:, :], ALU.mult, ALU.add))

            dve.wait_ge(s_x, 16)
            for t in range(T):
                ins = dve.bn_stats(stats[:, t, :], xs[:, t, :])
            link(ins)
            for t in range(T):
                ins = dve.bn_aggr(mv[:, t, :], stats[:, t, :])
            link(ins)
            dve.tensor_scalar(mv[:, :, 1], mv[:, :, 1], EPS, None, ALU.add).then_inc(s_var, 1)
            dve.wait_ge(s_std, 1)
            link(dve.reciprocal(norm[:, :, 0], std[:, :]))
            dve.scalar_tensor_tensor(norm[:, :, 1], mv[:, :, 0], -1.0, norm[:, :, 0],
                                     ALU.mult, ALU.mult).then_inc(s_norm, 1)

            def onehots(slot, picked, first, done):
                for j in range(GROUP):
                    c = first + j
                    dve.tensor_scalar(rows[:, slot, j, :], iota[:, 0:P], picked[:, 0, c:c + 1],
                                      picked[:, 1, c:c + 1], ALU.is_equal, ALU.mult)
                    ins = dve.tensor_scalar(cols[:, slot, j, :], iota[:, :], picked[:, 2, c:c + 1],
                                            None, ALU.is_equal)
                ins.then_inc(done, 1)

            def add_to_adj(bank, first, done):
                window = adj[:, :, bass.ds(first, WINDOW)]
                dve.tensor_tensor(window, bank[:, 0:COLS].rearrange("p (b w) -> p b w", w=WINDOW), window,
                                  ALU.add).then_inc(done, 1)

            dve.wait_ge(s_const, 3)
            dve.wait_ge(s_adj_zero, 1)
            dve.sem_inc(s_flush, 1)

            def pair_of_tiles(i):
                for a, edges in enumerate((src_lo, edge_w_sb[:, :], col[:, :])):
                    ins = dve.tensor_copy(now[:, a, :], edges[:, bass.ds(i * (PER_PAIR * GROUP), PER_PAIR * GROUP)])
                ins.then_inc(s_now, 1)
                dve.wait_ge(s_now, i + 1)

                def flush(g):
                    n = i * PER_PAIR + g
                    dve.wait_ge(s_group, n + 1)
                    dve.wait_ge(s_flush, n + 1)
                    first = nc.values_load(base_i[0:1, bass.ds(n, 1)], engines=[DVE], min_val=0, max_val=TOK,
                                           skip_runtime_bounds_check_because="destinations are nodes")
                    add_to_adj(edge_bank[g % 2], first, s_flush)

                def take_trans(u):
                    t = i * 2 + u
                    dve.wait_ge(s_proj, t * 3 + 2)
                    dve.wait_ge(s_trans_free, t + 1)
                    dve.tensor_tensor(trans, proj_bank[1][:, :], b_gnn_sb[:, 1, :], ALU.add).then_inc(s_trans, 1)
                    dve.wait_ge(s_trans, t + 1)
                    dve.sem_inc(s_bank_free[1], 1)

                def take_gate(u):
                    t = i * 2 + u
                    dve.wait_ge(s_proj, t * 3 + 3)
                    dve.tensor_tensor(tile(gate, t), proj_bank[2][:, :], b_gnn_sb[:, 2, :],
                                      ALU.add).then_inc(s_gate_in, 1)
                    dve.wait_ge(s_gate_in, t + 1)
                    dve.sem_inc(s_bank_free[2], 1)

                for g in range(PER_PAIR):
                    if g >= 2:
                        flush(g - 2)
                    onehots(g % 2, now, g * GROUP, s_onehot)
                    if g == 9:
                        take_trans(0)
                    if g == 13:
                        take_gate(0)
                take_trans(1)
                flush(PER_PAIR - 2)
                flush(PER_PAIR - 1)
                take_gate(1)

            dve.wait_ge(s_filled, 16 * 3)
            dve.wait_ge(s_small, 16 * 6)
            with dve.Fori(0, PAIRS) as i:
                pair_of_tiles(i)

            dve.wait_ge(s_count, 1)
            dve.tensor_scalar(strays_i[:, :], misc_bank[0:1, 0:1], 1.0, None, ALU.min).then_inc(s_branch, 1)
            dve.wait_ge(s_branch, 1)
            found = nc.values_load(strays_i[0:1, 0:1], engines=[DVE], min_val=0, max_val=1)
            with dve.If(found == 0):
                dve.nop()
            with dve.Else():
                dve.memset(adj[:, :, :], 0.0).then_inc(s_redo, 1)
                dve.wait_ge(s_redo, 1)
                with dve.Fori(0, WINDOWS) as w:
                    dve.tensor_copy(col[:, :], dst_f).then_inc(s_redo, 1)
                    dve.wait_ge(s_redo, w * 6 + 2)
                    dve.tensor_scalar(outside[:, :], col[:, :], float(WINDOW), None, ALU.is_ge)
                    dve.tensor_scalar(below[:, :], col[:, :], 0.0, None, ALU.is_lt).then_inc(s_redo, 1)
                    dve.wait_ge(s_redo, w * 6 + 3)
                    dve.tensor_tensor(outside[:, :], outside[:, :], below[:, :], ALU.add).then_inc(s_redo, 1)
                    dve.wait_ge(s_redo, w * 6 + 4)
                    dve.tensor_tensor(col[:, :], col[:, :], block_col, ALU.add).then_inc(s_redo, 1)
                    dve.wait_ge(s_redo, w * 6 + 5)
                    dve.scalar_tensor_tensor(col[:, :], outside[:, :], float(2 * TOK), col[:, :],
                                             ALU.mult, ALU.add)
                    dve.tensor_scalar(dst_f, dst_f, -float(WINDOW), None, ALU.add).then_inc(s_redo, 2)
                    dve.wait_ge(s_redo, w * 6 + 7)
                    settle(dve)
                    with dve.Fori(0, GROUPS) as g:
                        n = w * GROUPS + g
                        for a, edges in enumerate((src_lo, edge_w_sb[:, :], col[:, :])):
                            ins = dve.tensor_copy(now[:, a, 0:GROUP], edges[:, bass.ds(g * GROUP, GROUP)])
                        ins.then_inc(s_redo_copy, 1)
                        dve.wait_ge(s_redo_copy, n + 1)
                        onehots(0, now, 0, s_redo_onehot)
                        dve.wait_ge(s_redo_group, n + 1)
                        add_to_adj(edge_bank[0], w * WINDOW, s_redo_flush)
                        dve.wait_ge(s_redo_flush, n + 1)

            def stage(t):
                dve.tensor_copy(adj_block[:, :], adj[:, bass.ds(t, 1), 0:TOK].rearrange("p a n -> p (a n)")
                                ).then_inc(s_adj_block, 1)

            dve.wait_ge(s_flush, GROUPS + 1)
            dve.wait_ge(s_trans_free, T + 1)
            stage(0)
            dve.wait_ge(s_adj_turn, 1)
            stage(1)

            def choose(t, u, first, last):
                step = t * 8
                dve.wait_ge(s_logits, t + 1)
                dve.tensor_tensor(logits[:, u, :], misc_bank[:, 256 + u * E:256 + (u + 1) * E], bg_sb[:, :],
                                  ALU.add).then_inc(s_pick, 1)
                dve.wait_ge(s_pick, step + 1)
                settle(dve)
                dve.max(best[:, u, :], logits[:, u, :]).then_inc(s_pick, 1)
                dve.wait_ge(s_pick, step + 2)
                settle(dve)
                dve.max_index(best_i[:, u, :], best[:, u, :], logits[:, u, :]).then_inc(s_pick, 1)
                dve.tensor_tensor(odds[:, u:u + 1], best[:, u, 1:2], best[:, u, 0:1], ALU.subtract).then_inc(s_gap, 1)
                dve.wait_ge(s_pick, step + 3)
                dve.tensor_copy(best_f[:, u, :], best_i[:, u, 0:TOP_K]).then_inc(s_pick, 1)
                dve.wait_ge(s_pick, step + 4)
                dve.tensor_tensor(hit[:, u, :, :], iota[:, 0:E].unsqueeze(1).broadcast_to([P, TOP_K, E]),
                                  best_f[:, u, :].unsqueeze(2).broadcast_to([P, TOP_K, E]),
                                  ALU.is_equal).then_inc(s_pick, 1)
                dve.wait_ge(s_pick, step + 5)
                dve.tensor_tensor(chosen[:, u, :], hit[:, u, 0, :], hit[:, u, 1, :], ALU.add).then_inc(s_pick, 1)
                dve.wait_ge(s_pick, step + 6)
                if last:
                    dve.tensor_scalar(chosen[:, u, :], chosen[:, u, :], real[:, :], None, ALU.mult).then_inc(s_pick, 1)
                    dve.wait_ge(s_pick, step + 7)
                if first:
                    dve.tensor_copy(chosen_sum[:, u, :], chosen[:, u, :]).then_inc(s_chosen, 1)
                else:
                    dve.wait_ge(s_chosen, t)
                    dve.tensor_tensor(chosen_sum[:, u, :], chosen_sum[:, 1 - u, :], chosen[:, u, :],
                                      ALU.add).then_inc(s_chosen, 1)
                if not last:
                    dve.sem_inc(s_pick, 2)

            def place(i, u, saved, last):
                t = i * 2 + u
                step = t * 5
                if saved:
                    dve.wait_ge(s_route_saved[u], i * (16 * TOP_K))
                dve.wait_ge(s_rank, t + 1)
                dve.tensor_tensor(hit_rank[:, u, :, :], hit[:, u, :, :],
                                  misc_bank[:, 320:320 + E].unsqueeze(1).broadcast_to([P, TOP_K, E]),
                                  ALU.mult).then_inc(s_placing, 1)
                dve.tensor_scalar(first_col[:, u, :], best_f[:, u, :], float(T), None, ALU.mult)
                dve.tensor_copy(route[:, u, :, 0], token_i[:, bass.ds(t, 1)].broadcast_to([P, TOP_K]))
                dve.wait_ge(s_odds, t + 1)
                dve.tensor_scalar(odds1[:, u:u + 1], odds[:, u:u + 1], 1.0, None, ALU.add).then_inc(s_place, 1)
                dve.wait_ge(s_place, step + 1)
                dve.tensor_reduce(rank[:, u, :], hit_rank[:, u, :, :], mybir.AxisListType.X, ALU.add)
                dve.reciprocal(route_score[:, u, 0, 1:2], odds1[:, u:u + 1]).then_inc(s_place, 1)
                dve.wait_ge(s_place, step + 2)
                dve.tensor_tensor(route_score[:, u, 1, 1:2], route_score[:, u, 0, 1:2], odds[:, u:u + 1], ALU.mult)
                dve.tensor_copy(rank_i[:, u, :], rank[:, u, :]).then_inc(s_place, 1)
                dve.wait_ge(s_place, step + 3)
                dve.scalar_tensor_tensor(row[:, u, :], rank[:, u, :], float(ROUTES), first_col[:, u, :],
                                         ALU.mult, ALU.add)
                dve.tensor_scalar(rank_tile_i[:, u, :], rank_i[:, u, :], 7, None,
                                  ALU.logical_shift_right).then_inc(s_place, 1)
                dve.wait_ge(s_place, step + 4)
                dve.tensor_copy(rank_tile[:, u, :], rank_tile_i[:, u, :]).then_inc(s_place, 1)
                dve.wait_ge(s_place, step + 5)
                if last:
                    link_last = dve.scalar_tensor_tensor(row[:, u, :], rank_tile[:, u, :], -float(P * ROUTES - 1),
                                                         row[:, u, :], ALU.mult, ALU.add)
                    link_last.then_inc(s_place, 1)
                    dve.wait_ge(s_place, T * 5 + 1)
                    dve.scalar_tensor_tensor(row_i[:, u, :, 0], row[:, u, :], real[:, :], unreal_row[:, :],
                                             ALU.mult, ALU.add).then_inc(s_routed, 1)
                else:
                    dve.scalar_tensor_tensor(row_i[:, u, :, 0], rank_tile[:, u, :], -float(P * ROUTES - 1),
                                             row[:, u, :], ALU.mult, ALU.add).then_inc(s_routed, 1)

            def finish(i, u, more, now_place, now_choose):
                t = i * 2 + u
                xt, gt = tile(xs, t), tile(gate, t)
                x1t = x1[:, u, :]
                dve.wait_ge(s_agg, t + 1)
                dve.wait_ge(s_x1y, t + 1)
                dve.tensor_tensor(x1t, agg_bank[u][:, :], b_gnn_sb[:, 0, :], ALU.add).then_inc(s_agg_free, 1)
                if now_place:
                    place(i - 1, u, now_place == 2, False)
                if more:
                    dve.wait_ge(s_adj_turn, t + 2)
                    settle(dve)
                    stage(t + 2)
                dve.wait_ge(s_agg_free, t + 3)
                dve.scalar_tensor_tensor(x1t, x1t, 0.0, gt, ALU.max, ALU.mult).then_inc(s_relu, 1)
                dve.wait_ge(s_relu, t + 1)
                dve.tensor_tensor(x1t, xt, x1t, ALU.add).then_inc(s_x1, 1)
                dve.wait_ge(s_x1, t + 1)
                dve.bn_stats(stats[:, u, :], x1t).then_inc(s_ln, 1)
                dve.wait_ge(s_ln, t * 2 + 1)
                settle(dve)
                dve.bn_aggr(mv2[:, u, :], stats[:, u, :]).then_inc(s_ln, 1)
                dve.wait_ge(s_ln, t * 2 + 2)
                dve.tensor_scalar(mv2[:, u, 1:2], mv2[:, u, 1:2], EPS, None, ALU.add).then_inc(s_var2, 1)
                dve.wait_ge(s_std2, t + 1)
                dve.reciprocal(norm2[:, u, 0:1], std2[:, u:u + 1]).then_inc(s_rec2, 1)
                dve.wait_ge(s_rec2, t + 1)
                dve.scalar_tensor_tensor(norm2[:, u, 1:2], mv2[:, u, 0:1], -1.0, norm2[:, u, 0:1],
                                         ALU.mult, ALU.mult).then_inc(s_norm2, 1)
                if now_choose:
                    choose(t - 1, 1 - u, now_choose == 1, False)

            dve.wait_ge(s_ahead, 4)
            finish(0, 0, True, 0, 0)
            finish(0, 1, True, 0, 1)
            finish(1, 0, True, 1, 2)
            finish(1, 1, True, 1, 2)
            with dve.Fori(2, PAIRS - 1) as i:
                for u in range(2):
                    finish(i, u, True, 2, 2)
            finish(PAIRS - 1, 0, False, 2, 2)
            finish(PAIRS - 1, 1, False, 2, 2)
            place(PAIRS - 1, 0, True, False)
            choose(T - 1, 1, False, True)
            place(PAIRS - 1, 1, True, True)

            dve.wait_ge(s_counts, 1)
            link(dve.tensor_reduce(most[:, :], misc_bank[0:1, 384:384 + E], mybir.AxisListType.X, ALU.max))
            dve.tensor_scalar(over_i[:, :], most[:, :], float(CAP), None, ALU.is_gt).then_inc(s_over, 1)

            def add_b2(e, bank_c, out_c, done):
                dve.tensor_tensor(out_c, bank_c[:, :], b2_sb[:, bass.ds(e, 1), :].rearrange("p a d -> p (a d)"),
                                  ALU.add).then_inc(done, 1)

            def scale(column, out_c, done):
                dve.tensor_scalar(out_c, out_c, table_score[:, bass.ds(column, 1), 1], None,
                                  ALU.mult).then_inc(done, 1)

            dve.wait_ge(s_table, 16)
            dve.wait_ge(s_b2, 16)
            with dve.Fori(0, E // 2) as i:
                for u in range(2):
                    e = i * 2 + u
                    dve.wait_ge(s_y_out_free, e + 1)
                    for c in range(CAP_TILES):
                        n = e * CAP_TILES + c
                        dve.wait_ge(s_down, n + 1)
                        add_b2(e, down_bank[c], y_out[:, u, c, :], s_taken)
                        dve.wait_ge(s_taken, n + 1 + CAP_TILES)
                        scale(e * T + c, y_out[:, u, c, :], s_scaled)

            def scale_more():
                for u in range(2):
                    dve.wait_ge(s_added[u], 16 * CAP_TILES * (E // 2))
                with dve.Fori(0, E) as e:
                    with dve.Fori(0, MORE) as c:
                        n = e * MORE + c
                        dve.wait_ge(s_more_down, n + 2)
                        add_b2(e, down_bank[0], y_out[:, 0, 0, :], s_more_taken)
                        dve.wait_ge(s_more_taken, n + 2)
                        scale(e * T + c + CAP_TILES, y_out[:, 0, 0, :], s_more_scaled)

            beyond_share(dve, DVE, scale_more)


def kernel(x, src, dst, edge_weight, L0_gnn_w1, L0_gnn_w2, L0_gnn_w3, L0_gnn_b1, L0_gnn_b2, L0_gnn_b3,
           L0_ffn_Wg, L0_ffn_bg, L0_ffn_W1, L0_ffn_b1, L0_ffn_W2, L0_ffn_b2):
    from concourse import bacc
    from concourse.bass_utils import run_bass_kernel_spmd

    x, src, dst, edge_weight = (np.asarray(a) for a in (x, src, dst, edge_weight))
    n, d = x.shape
    tiles, pairs, per_pair, groups = split_shapes(n, len(src))
    slots = groups * GROUP * P
    more = slots - len(src)

    def by_tile(a):
        return np.ascontiguousarray(a.reshape(groups * GROUP, P).T)

    src_p = np.pad(src, (0, more), mode="edge")
    dst_p = np.pad(dst, (0, more), mode="edge")
    e, _, f = np.shape(L0_ffn_W1)
    arrays = {
        "x": np.pad(x, ((0, tiles * P - n), (0, 0))),
        "src": by_tile(src_p),
        "dst": by_tile(dst_p),
        "first_dst": np.ascontiguousarray(dst_p[:: GROUP * P][None, :]),
        "edge_w": by_tile(np.pad(edge_weight, (0, more))),
        "w_gnn": np.stack([L0_gnn_w1, L0_gnn_w2, L0_gnn_w3]),
        "b_gnn": np.stack([L0_gnn_b1, L0_gnn_b2, L0_gnn_b3]),
        "wg": np.asarray(L0_ffn_Wg),
        "bg": np.asarray(L0_ffn_bg)[None, :],
        "w1": np.asarray(L0_ffn_W1),
        "b1": np.ascontiguousarray(np.asarray(L0_ffn_b1).reshape(e, f // P, P).transpose(2, 1, 0)),
        "w2": np.asarray(L0_ffn_W2),
        "b2": np.ascontiguousarray(np.asarray(L0_ffn_b2).reshape(1, -1)),
    }
    nc = bacc.Bacc("TRN2", target_bir_lowering=False, num_devices=1)
    args = {
        name: nc.dram_tensor(f"in_{name}", a.shape, mybir.dt.from_np(a.dtype), kind="ExternalInput").ap()
        for name, a in arrays.items()
    }
    rows = (tiles + CAP_TILES) * P
    out = nc.dram_tensor("out", (rows, d), F32, kind="ExternalOutput").ap()
    y_rows = nc.dram_tensor("y_rows", (rows, d), F32, kind="Internal").ap()
    routes = nc.dram_tensor("routes", (P * e * tiles + P * TOP_K, 2), I32, kind="Internal").ap()
    gnn_moe_layer(nc, out=out, y_rows=y_rows, routes=routes, n_nodes=n, **args)
    r = run_bass_kernel_spmd(nc, [{f"in_{name}": a for name, a in arrays.items()}], core_ids=[0])
    return r.results[0]["out"][:n]
```

```python
from contextlib import ExitStack

import numpy as np

import concourse.bass as bass
from concourse import mybir

ALU = mybir.AluOpType
ACT = mybir.ActivationFunctionType
F32 = mybir.dt.float32
F32R = mybir.dt.float32r
I32 = mybir.dt.int32
U32 = mybir.dt.uint32
DVE = mybir.EngineType.DVE
PE = mybir.EngineType.PE

P = 128
GROUP = 3
WINDOW = 15
EPS = 1e-5
TOP_K = 2
SLOTS = 3
CAP_TILES = 3


def split_shapes(n_nodes, n_edges):
    tiles = -(-n_nodes // P)
    tiles += tiles % 2
    pairs = tiles // 2
    groups = -(-n_edges // (P * GROUP))
    per_pair = -(-(groups - SLOTS) // pairs)
    per_pair = -(-per_pair // SLOTS) * SLOTS
    return tiles, pairs, per_pair, per_pair * pairs + SLOTS


def gnn_moe_layer(nc, x, src, dst, first_dst, edge_w, w_gnn, b_gnn, wg, bg, w1, b1, w2, b2, out, y_rows,
                  routes, n_nodes):
    D = x.shape[1]
    KD = D // P
    E, _, F = w1.shape
    KF = F // P
    T = x.shape[0] // P
    PAIRS = T // 2
    TOK = T * P
    NB = T
    GROUPS = first_dst.shape[1]
    EDGE_TILES = GROUPS * GROUP
    PER_PAIR = (GROUPS - SLOTS) // PAIRS
    COLS = NB * WINDOW
    WINDOWS = -(-TOK // WINDOW)
    ROUTES = E * T
    CAP = CAP_TILES * P
    assert D == 512 and COLS <= 512 and E <= 8
    assert T % 2 == 0 and 10 <= T <= 12 and (T - 1) * P < n_nodes <= TOK
    assert PER_PAIR % SLOTS == 0 and 21 <= PER_PAIR <= 3 * KD * 6

    ctx = ExitStack()
    with ctx:

        def sb(name, shape, dt=F32):
            return ctx.enter_context(nc.sbuf_tensor(name, shape, dt))

        def ps(name, shape):
            return ctx.enter_context(nc.psum_tensor(name, shape, F32))

        def sem(name):
            return ctx.enter_context(nc.semaphore(name))

        ident = sb("ident", [P, P])
        iota = sb("iota", [P, COLS])
        ones = sb("ones", [P, P])
        ones_col = ones[:, 0:1]
        before = sb("before", [P, P])
        real = sb("real", [P, 1])
        unreal_row = sb("unreal_row", [P, TOP_K])
        token_i = sb("token_i", [P, T], I32)
        xs = sb("xs", [P, T, D])
        gate = sb("gate", [P, T, D])
        b_gnn_sb = sb("b_gnn_sb", [P, 3, D])
        xn = sb("xn", [P, 2, D])
        xT_lo = sb("xT_lo", [P, 2, KD * P], F32R)
        pair = sb("pair", [P, 2, D])
        trans, keep = pair[:, 0, :], pair[:, 1, :]
        x1 = pair
        mv2 = sb("mv2", [P, 2, 2])
        std2 = sb("std2", [P, 2])
        norm2 = sb("norm2", [P, 2, 2])
        stats = sb("stats", [P, T, 6])
        mv = sb("mv", [P, T, 2])
        std = sb("std", [P, T])
        norm = sb("norm", [P, T, 2])
        edges = sb("edges", [P, 4 * EDGE_TILES])
        edge_w_sb, outside, below, col = (edges[:, n * EDGE_TILES:(n + 1) * EDGE_TILES] for n in range(4))
        adj_block = edges[:, 0:TOK]
        src_i = sb("src_i", [P, EDGE_TILES], I32)
        dst_i = sb("dst_i", [P, EDGE_TILES], I32)
        base_i = sb("base_i", [P, GROUPS], I32)
        src_lo = src_i[:, :].bitcast(F32)
        dst_f = dst_i[:, :].bitcast(F32)
        block_i = sb("block_i", [P, EDGE_TILES], I32)
        block_col = block_i[:, :].bitcast(F32)
        strays = sb("strays", [P, 1])
        strays_i = sb("strays_i", [1, 1], I32)
        now = sb("now", [P, 3, PER_PAIR * GROUP])
        wg_sb = sb("wg_sb", [P, KD, E])
        bg_sb = sb("bg_sb", [P, E])
        b1_sb = sb("b1_sb", [P, KF, E])
        logits = sb("logits", [P, 2, E])
        best = sb("best", [P, 2, 8])
        best_i = sb("best_i", [P, 2, 8], U32)
        best_f = sb("best_f", [P, 2, TOP_K])
        odds = sb("odds", [P, 2])
        odds1 = sb("odds1", [P, 2])
        hit = sb("hit", [P, 2, TOP_K, E])
        chosen = sb("chosen", [P, 2, E])
        chosen_sum = sb("chosen_sum", [P, 2, E])
        hit_rank = sb("hit_rank", [P, 2, TOP_K, E])
        rank = sb("rank", [P, 2, TOP_K])
        rank_i = sb("rank_i", [P, 2, TOP_K], I32)
        rank_tile_i = sb("rank_tile_i", [P, 2, TOP_K], I32)
        rank_tile = sb("rank_tile", [P, 2, TOP_K])
        first_col = sb("first_col", [P, 2, TOP_K])
        row = sb("row", [P, 2, TOP_K])
        row_i = sb("row_i", [P, 2, TOP_K, 1], I32)
        route = sb("route", [P, 2, TOP_K, 2], I32)
        route_score = route[:, :, :, :].rearrange("p u j a -> p (u j a)").bitcast(F32).rearrange(
            "p (u j a) -> p u j a", u=2, a=2)
        table = sb("table", [P, ROUTES, 2], I32)
        table_score = table[:, :, :].rearrange("p r a -> p (r a)").bitcast(F32).rearrange("p (r a) -> p r a", a=2)
        most = sb("most", [1, 1])
        over_i = sb("over_i", [1, 1], I32)
        get_token = sb("get_token", [P, 2, CAP_TILES], I32)
        put_token = sb("put_token", [P, 2, CAP_TILES], I32)

        def in_turn(name, firsts, seconds):
            with ExitStack() as early:
                made = [early.enter_context(nc.sbuf_tensor(*t)) for t in firsts]
            made += [sb(*t) for t in seconds]

            def words(tensors):
                return sum(int(np.prod(shape[1:])) for _, shape, _ in tensors)

            left = words(firsts) - words(seconds)
            if left > 0:
                sb(name + "_left", [P, left])
            return made

        expert_size = KD * F + KF * D
        support, w_sb = in_turn("support", [("support", [P, T, D], F32)],
                                [("w_sb", [P, 2, expert_size], F32)])
        adj, *expert_parts = in_turn(
            "adj", [("adj", [P, NB, TOK + WINDOW], F32)],
            [(f"{name}_{part}", shape, F32R) for part in ("hi", "lo") for name, shape in (
                ("ew", [P, 2, expert_size]), ("y_inT", [P, KD, CAP]), ("hT", [P, KF, CAP]))])
        (ew_hi, yi_hi, h_hi), (ew_lo, yi_lo, h_lo) = expert_parts[0:3], expert_parts[3:6]

        of_up, of_down = slice(0, KD * F), slice(KD * F, expert_size)

        def up_weights(w, u):
            return w[:, u, 0:KD * F].rearrange("p (k f) -> p k f", k=KD)

        def down_weights(w, u):
            return w[:, u, KD * F:].rearrange("p (f d) -> p f d", f=KF)

        rows, cols, adjT_lo = in_turn(
            "onehots", [("rows", [P, SLOTS, GROUP, P], F32), ("cols", [P, SLOTS, GROUP, COLS], F32)],
            [("adjT_lo", [P, 2, NB * P], F32R)])
        xT_hi, yT = in_turn("turned", [("xT_hi", [P, 2, KD * P], F32R)], [("yT", [P, 2, KD * P], F32)])
        parts = [("sup_hi", [P, NB, D], F32R), ("sup_lo", [P, NB, D], F32R), ("adjT_hi", [P, 2, NB * P], F32R)]
        w_parts = [("w_hi", [P, 3 * KD * D], F32R), ("w_lo", [P, 3 * KD * D], F32R),
                   ("w_left", [P, 2 * NB * D + 2 * NB * P - 6 * KD * D], F32R)]
        with ExitStack() as early:
            w_hi, w_lo, _ = (early.enter_context(nc.sbuf_tensor(*t))[:, :] for t in w_parts)
        sup_hi, sup_lo, adjT_hi, b2_sb, y_in, y_out, hT, more_inT = in_turn("parts", parts, [
            ("b2_sb", [P, E, D], F32), ("y_in", [P, 2, CAP_TILES, D], F32), ("y_out", [P, 2, CAP_TILES, D], F32),
            ("hT", [P, KF, CAP], F32), ("more_inT", [P, KD, P], F32)])
        w_hi, w_lo = (w.rearrange("p (m k n) -> p m k n", m=3, k=KD) for w in (w_hi, w_lo))
        w_raw = [support[:, 0:4, :], support[:, 4:8, :], gate[:, 4:8, :]]

        bank = [ps(f"bank{i}", [P, 512]) for i in range(8)]
        turn_bank = bank[0:2]
        proj_bank = bank[2:5]
        edge_bank = bank[5:8]
        misc_bank = bank[7]
        count_bank = bank[7]
        agg_bank = bank[2:4]
        adj_bank = bank[4:7]
        in_bank = [bank[0], bank[1], bank[7]]
        up_bank = bank[2:4]
        down_bank = bank[4:7]

        s_x = [sem("s_x_first"), sem("s_x_second")]
        s_edges = sem("s_edges")
        s_wproj = [sem(f"s_wproj{m}") for m in range(3)]
        s_small = sem("s_small")
        s_expert = [sem("s_expert_even"), sem("s_expert_odd")]
        s_zero = sem("s_zero")
        s_const = sem("s_const")
        s_adj_zero = sem("s_adj_zero")
        s_chain = sem("s_chain")
        s_var = sem("s_var")
        s_std = sem("s_std")
        s_norm = sem("s_norm")
        s_xn = sem("s_xn")
        s_turn = sem("s_turn")
        s_xT_hi = sem("s_xT_hi")
        s_xT = sem("s_xT")
        s_w_hi = sem("s_w_hi")
        s_w_lo = [sem(f"s_w_lo{m}") for m in range(3)]
        s_proj = sem("s_proj")
        s_support = sem("s_support")
        s_trans = sem("s_trans")
        s_gate_in = sem("s_gate_in")
        s_trans_free = sem("s_trans_free")
        s_gate = sem("s_gate")
        s_mix = sem("s_mix")
        s_onehot = sem("s_onehot")
        s_weighted = sem("s_weighted")
        s_group = sem("s_group")
        s_flush = sem("s_flush")
        s_strays = sem("s_strays")
        s_count = sem("s_count")
        s_branch = sem("s_branch")
        s_redo = sem("s_redo")
        s_redo_onehot = sem("s_redo_onehot")
        s_redo_group = sem("s_redo_group")
        s_redo_flush = sem("s_redo_flush")
        s_now = sem("s_now")
        s_redo_copy = sem("s_redo_copy")
        s_rec2 = sem("s_rec2")
        s_adj_block = sem("s_adj_block")
        s_adj_turn = sem("s_adj_turn")
        s_adjT_hi = sem("s_adjT_hi")
        s_adjT = sem("s_adjT")
        s_sup_hi = sem("s_sup_hi")
        s_sup_lo = [sem("s_sup_lo_gpsimd"), sem("s_sup_lo_vector")]
        s_agg = sem("s_agg")
        s_relu = sem("s_relu")
        s_agg_free = sem("s_agg_free")
        s_x1 = sem("s_x1")
        s_ln = sem("s_ln")
        s_var2 = sem("s_var2")
        s_std2 = sem("s_std2")
        s_norm2 = sem("s_norm2")
        s_y = sem("s_y")
        s_turn2 = sem("s_turn2")
        s_yT = sem("s_yT")
        s_x1y = sem("s_x1y")
        s_y_saved = [sem("s_y_saved_even"), sem("s_y_saved_odd")]
        s_out = sem("s_out")
        s_zeros = sem("s_zeros")
        s_ahead = sem("s_ahead")
        s_filled = sem("s_filled")
        s_b2 = sem("s_b2")
        s_logits = sem("s_logits")
        s_pick = sem("s_pick")
        s_gap = sem("s_gap")
        s_odds = sem("s_odds")
        s_chosen = sem("s_chosen")
        s_rank = sem("s_rank")
        s_placing = sem("s_placing")
        s_place = sem("s_place")
        s_routed = sem("s_routed")
        s_route_saved = [sem("s_route_saved_even"), sem("s_route_saved_odd")]
        s_table = sem("s_table")
        s_counts = sem("s_counts")
        s_over = sem("s_over")
        s_get_token = sem("s_get_token")
        s_got = [[sem(f"s_got_{u}_{c}") for c in range(CAP_TILES)] for u in ("even", "odd")]
        s_in_turned = sem("s_in_turned")
        s_y_hi = sem("s_y_hi")
        s_y_inT = sem("s_y_inT")
        s_ew_hi = sem("s_ew_hi")
        s_ew_lo = sem("s_ew_lo")
        s_gelu = sem("s_gelu")
        s_h_hi = sem("s_h_hi")
        s_up = sem("s_up")
        s_h = sem("s_h")
        s_down = sem("s_down")
        s_taken = sem("s_taken")
        s_scaled = sem("s_scaled")
        s_put_token = sem("s_put_token")
        s_y_out_free = sem("s_y_out_free")
        s_added = [sem("s_added_even"), sem("s_added_odd")]
        s_more_expert = sem("s_more_expert")
        s_more_token = sem("s_more_token")
        s_more_got = sem("s_more_got")
        s_more_turned = sem("s_more_turned")
        s_more_inT = sem("s_more_inT")
        s_more_up = sem("s_more_up")
        s_more_h = sem("s_more_h")
        s_more_down = sem("s_more_down")
        s_more_taken = sem("s_more_taken")
        s_more_scaled = sem("s_more_scaled")
        s_more_added = sem("s_more_added")
        s_settled = sem("s_settled")

        block = ctx.enter_context(nc.Block())

        def tile(a, t):
            return a[:, bass.ds(t, 1), :].rearrange("p a d -> p (a d)")

        def one(a, t, j):
            return a[:, bass.ds(t, 1), j]

        def split_support(eng, k, done):
            eng.tensor_tensor(sup_lo[:, k, :], support[:, k, :], sup_hi[:, k, :].bitcast(F32),
                              ALU.subtract).then_inc(done, 1)

        def settle(eng):
            eng.sem_inc(s_settled, 1)

        MORE = T - CAP_TILES

        def beyond_share(eng, kind, body):
            eng.wait_ge(s_over, 1)
            over = nc.values_load(over_i[0:1, 0:1], engines=[kind], min_val=0, max_val=1)
            with eng.If(over == 0):
                eng.nop()
            with eng.Else():
                body()

        @block.sync
        def _(sp):
            sp.dma_start(dst_i[:, :], dst).then_inc(s_edges, 16)
            sp.dma_start(base_i[:, :], first_dst.broadcast_to([P, GROUPS])).then_inc(s_edges, 16)
            sp.dma_start(src_i[:, :], src).then_inc(s_edges, 16)
            sp.dma_start(edge_w_sb[:, :], edge_w).then_inc(s_edges, 16)
            for h in range(2):
                half = slice(h * PAIRS, (h + 1) * PAIRS)
                sp.dma_start(xs[:, half, :], x.rearrange("(t p) d -> p t d", p=P)[:, half, :]).then_inc(s_x[h], 16)
            for m in range(3):
                sp.dma_start(w_raw[m], w_gnn[m].rearrange("(k p) n -> p k n", p=P)).then_inc(s_wproj[m], 16)
            for m in range(3):
                sp.dma_start(b_gnn_sb[:, m, :], b_gnn[m:m + 1, :].broadcast_to([P, D])).then_inc(s_small, 16)
            sp.dma_start(wg_sb[:, :, :], wg.rearrange("(k p) e -> p k e", p=P)).then_inc(s_small, 16)
            sp.dma_start(bg_sb[:, :], bg.broadcast_to([P, E])).then_inc(s_small, 16)
            sp.dma_start(b1_sb[:, :, :], b1).then_inc(s_small, 16)

            def load_expert(e, u, done):
                sp.dma_start(up_weights(w_sb, u),
                             w1[bass.ds(e, 1)].rearrange("a (k p) f -> p (a k) f", p=P)).then_inc(done, 16)
                sp.dma_start(down_weights(w_sb, u),
                             w2[bass.ds(e, 1)].rearrange("a (k p) n -> p (a k) n", p=P)).then_inc(done, 16)

            sp.wait_ge(s_zeros, 1)
            for rows_out in (y_rows, out):
                sp.dma_start(rows_out[TOK:TOK + CAP, :].rearrange("(c p) d -> p c d", p=P),
                             gate[:, 0:CAP_TILES, :]).then_inc(s_filled, 16)
            sp.wait_ge(s_ahead, 1)
            sp.dma_start(routes[0:P * ROUTES, :].rearrange("(p r) a -> p (r a)", p=P),
                         table[:, :, :].rearrange("p r a -> p (r a)")).then_inc(s_filled, 16)
            sp.wait_ge(s_sup_lo[0], NB - 2)
            sp.wait_ge(s_sup_lo[1], 2)
            load_expert(0, 0, s_expert[0])
            load_expert(1, 1, s_expert[1])
            with sp.Fori(0, PAIRS) as i:
                for u in range(2):
                    t = i * 2 + u
                    sp.wait_ge(s_y, t + 1)
                    sp.dma_start(y_rows[bass.ds(t * P, P), :], xn[:, u, :]).then_inc(s_y_saved[u], 16)
                    sp.wait_ge(s_x1y, t + 3)
                    sp.dma_start(out[bass.ds(t * P, P), :], tile(xs, t)).then_inc(s_out, 16)
            sp.wait_ge(s_agg, T)
            sp.dma_start(b2_sb[:, :, :].rearrange("p e d -> p (e d)"),
                         b2.broadcast_to([P, E * D])).then_inc(s_b2, 16)
            for u in range(2):
                sp.wait_ge(s_route_saved[u], 16 * TOP_K * PAIRS)
            sp.dma_start(table[:, :, :].rearrange("p r a -> p (r a)"),
                         routes[0:P * ROUTES, :].rearrange("(p r) a -> p (r a)", p=P)).then_inc(s_table, 16)
            for c in range(CAP_TILES):
                sp.wait_ge(s_got[0][c], 16)
            with sp.Fori(0, E // 2 - 1) as i:
                for u in range(2):
                    e = i * 2 + u
                    sp.wait_ge(s_ew_lo, e * 2 + 2)
                    load_expert(e + 2, u, s_expert[u])

            def load_more():
                sp.wait_ge(s_ew_lo, E * 2)
                with sp.Fori(0, E) as e:
                    sp.wait_ge(s_more_down, e * MORE + 1)
                    load_expert(e, 0, s_more_expert)

            beyond_share(sp, mybir.EngineType.SP, load_more)
            for u in range(2):
                sp.wait_ge(s_added[u], 16 * CAP_TILES * (E // 2))

        @block.gpsimd
        def _(pool):
            pool.memset(ident[:, :], 0.0).then_inc(s_zero, 1)
            pool.iota(iota[:, :], [[1, COLS]], base=0, channel_multiplier=0,
                      allow_small_or_imprecise_dtypes=True).then_inc(s_const, 1)
            pool.memset(ones[:, :], 1.0).then_inc(s_const, 1)
            pool.wait_ge(s_zero, 1)
            pool.affine_select(out=ident[:, :], in_=ident[:, :], compare_op=ALU.not_equal, fill=1.0,
                               base=0, pattern=[[-1, P]], channel_multiplier=1).then_inc(s_const, 1)
            pool.memset(adj[:, :, :], 0.0).then_inc(s_adj_zero, 1)
            pool.memset(gate[:, 0:CAP_TILES, :], 0.0).then_inc(s_zeros, 1)
            pool.memset(table[:, :, :], 0).then_inc(s_zero, 1)
            pool.wait_ge(s_zero, 2)
            token_of = table[:, :, :].rearrange("p (e c) a -> p e c a", e=E)
            for c in range(CAP_TILES):
                last = T if c == CAP_TILES - 1 else c + 1
                ins = pool.iota(token_of[:, :, c:last, 0], [[0, E], [0, last - c]], base=TOK + c * P,
                                channel_multiplier=1)
                ins.then_inc(s_zero, 1)
            pool.wait_ge(s_zero, 2 + CAP_TILES)
            pool.iota(token_i[:, :], [[P, T]], base=0, channel_multiplier=1).then_inc(s_ahead, 1)
            nodes = n_nodes - (T - 1) * P
            pool.memset(real[:, :], 1.0).then_inc(s_zero, 1)
            pool.iota(unreal_row[:, :], [[1, TOP_K]], base=P * ROUTES, channel_multiplier=TOP_K,
                      allow_small_or_imprecise_dtypes=True).then_inc(s_zero, 1)
            pool.wait_ge(s_const, 3)
            pool.affine_select(out=before[:, :], in_=ones[:, :], compare_op=ALU.is_gt, fill=0.0,
                               base=0, pattern=[[1, P]], channel_multiplier=-1).then_inc(s_ahead, 1)
            pool.wait_ge(s_zero, 4 + CAP_TILES)
            pool.affine_select(out=real[:, :], in_=real[:, :], compare_op=ALU.is_gt, fill=0.0,
                               base=nodes, pattern=[[0, 1]], channel_multiplier=-1).then_inc(s_ahead, 1)
            pool.affine_select(out=unreal_row[:, :], in_=unreal_row[:, :], compare_op=ALU.is_ge, fill=0.0,
                               base=-nodes, pattern=[[0, TOP_K]], channel_multiplier=1).then_inc(s_ahead, 1)

            for m in range(3):
                pool.wait_ge(s_w_hi, m + 1)
                pool.tensor_tensor(w_lo[:, m, :, :], w_raw[m], w_hi[:, m, :, :].bitcast(F32),
                                   ALU.subtract).then_inc(s_w_lo[m], 1)

            with pool.Fori(0, PAIRS) as i:
                for u in range(2):
                    t = i * 2 + u
                    xt, gt = tile(xs, t), tile(gate, t)
                    pool.wait_ge(s_trans, t + 2)
                    pool.wait_ge(s_gate, t + 1)
                    pool.tensor_tensor(keep, trans, gt, ALU.mult).then_inc(s_mix, 1)
                    pool.wait_ge(s_mix, t * 2 + 1)
                    pool.tensor_tensor(keep, trans, keep, ALU.subtract).then_inc(s_mix, 1)
                    pool.wait_ge(s_mix, t * 2 + 2)
                    pool.tensor_tensor(xt, xt, keep, ALU.add).then_inc(s_trans_free, 1)

            for k in range(NB - 2):
                pool.wait_ge(s_sup_hi, k // 2 + 1)
                split_support(pool, k, s_sup_lo[0])

            def add_y(t, u):
                pool.wait_ge(s_y, t + 1)
                pool.tensor_tensor(tile(xs, t), x1[:, u, :], xn[:, u, :], ALU.add).then_inc(s_x1y, 1)

            def save_routes(t, u):
                pool.wait_ge(s_routed, t + 1)
                settle(pool)
                for j in range(TOP_K):
                    pool.indirect_dma_start(routes[:, :], bass.IndirectOffsetOnAxis(ap=row_i[:, u, j, :], axis=0),
                                            route[:, u, j, :], None).then_inc(s_route_saved[u], 16)

            add_y(0, 0)
            add_y(1, 1)
            pool.wait_ge(s_filled, 16 * 3)
            with pool.Fori(1, PAIRS) as i:
                for u in range(2):
                    save_routes(i * 2 + u - 2, u)
                    add_y(i * 2 + u, u)
            save_routes(T - 2, 0)
            save_routes(T - 1, 1)

            def get(e, i, u):
                pool.tensor_copy(get_token[:, u, :], table[:, bass.ds(e * T, CAP_TILES), 0]).then_inc(s_get_token, 1)
                pool.wait_ge(s_get_token, e + 1)
                settle(pool)
                for c in range(CAP_TILES):
                    pool.indirect_dma_start(y_in[:, u, c, :], None, y_rows[:, :],
                                            bass.IndirectOffsetOnAxis(ap=get_token[:, u, c:c + 1], axis=0)
                                            ).then_inc(s_got[u][c], 16)

            def put(e, i, u, first=False):
                pool.tensor_copy(put_token[:, u, :], table[:, bass.ds(e * T, CAP_TILES), 0]).then_inc(s_put_token, 1)
                pool.wait_ge(s_put_token, e + 1)
                pool.wait_ge(s_scaled, e * CAP_TILES + CAP_TILES)
                if not first:
                    pool.wait_ge(s_added[1 - u], (i + u) * (16 * CAP_TILES))
                pool.sem_inc(s_y_out_free, 1)
                for c in range(CAP_TILES):
                    pool.indirect_dma_start(out[:, :], bass.IndirectOffsetOnAxis(ap=put_token[:, u, c:c + 1], axis=0),
                                            y_out[:, u, c, :], None, compute_op=ALU.add).then_inc(s_added[u], 16)

            for u in range(2):
                pool.wait_ge(s_y_saved[u], 16 * PAIRS)
            pool.wait_ge(s_table, 16)
            get(0, 0, 0)
            get(1, 0, 1)
            pool.wait_ge(s_out, 16 * T)

            def put_and_get(i, u, first):
                e = i * 2 + u
                pool.wait_ge(s_in_turned, e * CAP_TILES + CAP_TILES)
                get(e + 2, i + 1, u)
                put(e, i, u, first)

            put_and_get(0, 0, True)
            put_and_get(0, 1, False)
            with pool.Fori(1, E // 2 - 1) as i:
                put_and_get(i, 0, False)
                put_and_get(i, 1, False)
            put(E - 2, E // 2 - 1, 0)
            put(E - 1, E // 2 - 1, 1)

            def move_more():
                for u in range(2):
                    pool.wait_ge(s_added[u], 16 * CAP_TILES * (E // 2))
                pool.wait_ge(s_in_turned, E * CAP_TILES)
                with pool.Fori(0, E) as e:
                    with pool.Fori(0, MORE) as c:
                        n = e * MORE + c
                        pool.tensor_copy(get_token[:, 0, 0:1],
                                         table[:, bass.ds(e * T + c + CAP_TILES, 1), 0]).then_inc(s_more_token, 1)
                        pool.wait_ge(s_more_token, n + 1)
                        settle(pool)
                        pool.indirect_dma_start(y_in[:, 0, 0, :], None, y_rows[:, :],
                                                bass.IndirectOffsetOnAxis(ap=get_token[:, 0, 0:1], axis=0)
                                                ).then_inc(s_more_got, 16)
                        pool.wait_ge(s_more_scaled, n + 1)
                        settle(pool)
                        pool.indirect_dma_start(out[:, :],
                                                bass.IndirectOffsetOnAxis(ap=get_token[:, 0, 0:1], axis=0),
                                                y_out[:, 0, 0, :], None, compute_op=ALU.add).then_inc(s_more_added, 16)
                        pool.wait_ge(s_more_added, n * 16 + 16)

            beyond_share(pool, mybir.EngineType.Pool, move_more)

        @block.scalar
        def _(act):
            act.sem_inc(s_support, 1)

            def normalize(t, u):
                act.activation(xn[:, u, :], tile(xs, t), ACT.Identity,
                               bias=one(norm, t, 1), scale=one(norm, t, 0)).then_inc(s_xn, 1)

            def turned(to, u, done):
                act.activation(to[:, u, :], turn_bank[u][:, :], ACT.Copy).then_inc(done, 1)

            def split_hi(m):
                act.wait_ge(s_wproj[m], 16)
                act.activation(w_hi[:, m, :, :], w_raw[m], ACT.Copy).then_inc(s_w_hi, 1)

            split_hi(0)

            act.wait_ge(s_var, 1)
            act.activation(std[:, :], mv[:, :, 1], ACT.Sqrt).then_inc(s_std, 1)
            split_hi(1)
            act.wait_ge(s_norm, 1)
            normalize(0, 0)
            normalize(1, 1)
            act.wait_ge(s_turn, 1)
            turned(xT_hi, 0, s_xT_hi)

            def project_pair(i, last):

                def keep_support(u):
                    t = i * 2 + u
                    act.wait_ge(s_proj, t * 3 + 1)
                    settle(act)
                    act.activation(tile(support, t), proj_bank[0][:, :], ACT.Copy).then_inc(s_support, 1)

                def keep_turned(u):
                    act.wait_ge(s_turn, i * 2 + u + 2)
                    turned(xT_hi, 1 - u, s_xT_hi)

                def open_gate(u):
                    t = i * 2 + u
                    act.wait_ge(s_gate_in, t + 2)
                    settle(act)
                    act.activation(tile(gate, t), tile(gate, t), ACT.Sigmoid).then_inc(s_gate, 1)
                    if not last:
                        normalize(t + 2, u)

                steps = {3: (keep_support, 0), 7: (keep_turned, 0), 12: (open_gate, 0), 14: (keep_support, 1)}
                if not last:
                    steps[18] = (keep_turned, 1)
                for g in range(PER_PAIR):
                    weight(i * PER_PAIR + g + SLOTS, (g + SLOTS) % PER_PAIR)
                    if g in steps:
                        step, u = steps[g]
                        step(u)
                open_gate(1)

            def weight(n, g):
                act.wait_ge(s_onehot, n + 1)
                for j in range(GROUP):
                    c = g * GROUP + j
                    ins = act.activation(rows[:, g % SLOTS, j, :], rows[:, g % SLOTS, j, :], ACT.Copy,
                                         scale=now[:, 1, c:c + 1])
                ins.then_inc(s_weighted, 1)

            for g in range(SLOTS):
                weight(g, g)
            split_hi(2)
            act.preload_act_table(ACT.Sigmoid)
            with act.Fori(0, PAIRS - 1) as i:
                project_pair(i, False)
            project_pair(PAIRS - 1, True)

            act.wait_ge(s_support, T + 1)
            act.wait_ge(s_proj, 3 * T)
            for k in range(0, NB, 2):
                act.activation(sup_hi[:, k:k + 2, :], support[:, k:k + 2, :], ACT.Copy).then_inc(s_sup_hi, 1)

            def turned_adj(t, u):
                for c in range(3):
                    act.wait_ge(s_adj_turn, t * 3 + c + 1)
                    n = min(4, NB - 4 * c)
                    act.activation(adjT_hi[:, u, 4 * c * P:(4 * c + n) * P], adj_bank[c][:, 0:n * P],
                                   ACT.Copy).then_inc(s_adjT_hi, 1)

            def normalize_y(i, u, more, route, last=False):
                t = i * 2 + u
                act.wait_ge(s_var2, t + 1)
                act.activation(std2[:, u:u + 1], mv2[:, u, 1:2], ACT.Sqrt).then_inc(s_std2, 1)
                act.wait_ge(s_norm2, t + 1)
                act.wait_ge(s_x1y, t + 1)
                if route:
                    act.wait_ge(s_y_saved[u], i * 16)
                act.activation(xn[:, u, :], x1[:, u, :], ACT.Identity,
                               bias=norm2[:, u, 1:2], scale=norm2[:, u, 0:1]).then_inc(s_y, 1)
                if more:
                    turned_adj(t + 2, u)
                if more == 2:
                    stage(t + 3)
                if route and not last:
                    exp_gap(t - 1, 1 - u)
                    act.preload_act_table(ACT.Sqrt)
                act.wait_ge(s_turn2, t + 1)
                turned(yT, u, s_yT)
                if last:
                    exp_gap(t - 1, 1 - u)

            def stage(t):
                act.wait_ge(s_adj_turn, t * 3)
                settle(act)
                act.activation(adj_block, adj[:, bass.ds(t, 1), 0:TOK].rearrange("p a n -> p (a n)"),
                               ACT.Copy).then_inc(s_adj_block, 1)

            def exp_gap(t, u):
                act.wait_ge(s_gap, t + 1)
                act.activation(odds[:, u:u + 1], odds[:, u:u + 1], ACT.Exp).then_inc(s_odds, 1)

            turned_adj(0, 0)
            act.preload_act_table(ACT.Sqrt)
            turned_adj(1, 1)
            stage(2)
            normalize_y(0, 0, 2, False)
            normalize_y(0, 1, 2, False)
            exp_gap(0, 0)
            act.preload_act_table(ACT.Sqrt)
            with act.Fori(1, PAIRS - 2) as i:
                for u in range(2):
                    normalize_y(i, u, 2, True)
            normalize_y(PAIRS - 2, 0, 2, True)
            normalize_y(PAIRS - 2, 1, 1, True)
            normalize_y(PAIRS - 1, 0, False, True)
            normalize_y(PAIRS - 1, 1, False, True, last=True)
            exp_gap(T - 1, 1)

            act.preload_act_table(ACT.Gelu)

            def split_weights_hi(u, half):
                act.activation(ew_hi[:, u, half], w_sb[:, u, half], ACT.Copy).then_inc(s_ew_hi, 1)

            def turned_in(e, c):
                act.wait_ge(s_in_turned, e * CAP_TILES + c + 1)
                act.activation(yi_hi[:, :, c * P:(c + 1) * P],
                               in_bank[c][:, :].rearrange("p (k n) -> p k n", k=KD), ACT.Copy).then_inc(s_y_hi, 1)

            def gelu(e, f, n):
                return act.activation(hT[:, f, 0:n], up_bank[f][:, 0:n], ACT.Gelu, bias=b1_sb[:, f, bass.ds(e, 1)])

            def expert(i, u, last):
                e = i * 2 + u
                if not last:
                    act.wait_ge(s_expert[1 - u], (i + u) * 32 + 32)
                    split_weights_hi(1 - u, of_up)
                for f in range(KF):
                    act.wait_ge(s_up, e * KF + f + 1)
                    settle(act)
                    gelu(e, f, CAP).then_inc(s_gelu, 1)
                    act.wait_ge(s_gelu, e * KF + f + 1)
                    act.activation(h_hi[:, f, :], hT[:, f, :], ACT.Copy).then_inc(s_h_hi, 1)
                if not last:
                    for c in range(CAP_TILES):
                        turned_in(e + 1, c)
                    split_weights_hi(1 - u, of_down)
                for c in range(CAP_TILES):
                    act.wait_ge(s_taken, e * CAP_TILES + c + 1 + CAP_TILES)
                    settle(act)
                    act.activation(y_out[:, u, c, :], y_out[:, u, c, :], ACT.Copy,
                                   scale=table_score[:, bass.ds(e * T + c, 1), 1]).then_inc(s_scaled, 1)

            act.wait_ge(s_adj_block, T)
            act.wait_ge(s_expert[0], 32)
            split_weights_hi(0, of_up)
            split_weights_hi(0, of_down)
            for c in range(CAP_TILES):
                turned_in(0, c)
            act.wait_ge(s_table, 16)
            with act.Fori(0, E // 2 - 1) as i:
                expert(i, 0, False)
                expert(i, 1, False)
            expert(E // 2 - 1, 0, False)
            expert(E // 2 - 1, 1, True)

            def gelu_more():
                with act.Fori(0, E) as e:
                    with act.Fori(0, MORE) as c:
                        n = e * MORE + c
                        act.wait_ge(s_more_turned, n + 1)
                        act.activation(more_inT[:, :, :], in_bank[0][:, :].rearrange("p (k n) -> p k n", k=KD),
                                       ACT.Copy).then_inc(s_more_inT, 1)
                        act.wait_ge(s_more_up, n + 1)
                        settle(act)
                        for f in range(KF):
                            ins = gelu(e, f, P)
                        ins.then_inc(s_more_h, 1)

            beyond_share(act, mybir.EngineType.Activation, gelu_more)

        @block.tensor
        def _(pe):
            def turn(u, done):
                for k in range(KD):
                    ins = pe.transpose(turn_bank[u][:, k * P:(k + 1) * P], xn[:, u, k * P:(k + 1) * P], ident[:, :])
                ins.then_inc(done, 1)

            def edge_products(bank, slot, done):
                for j in range(GROUP):
                    ins = pe.matmul(bank[:, 0:COLS], rows[:, slot, j, :], cols[:, slot, j, :],
                                    start=(j == 0), stop=(j == GROUP - 1))
                ins.then_inc(done, 1)

            pe.wait_ge(s_const, 3)
            pe.wait_ge(s_strays, 1)
            pe.matmul(count_bank[0:1, 0:1], strays[:, :], ones_col[:, :], start=True, stop=True).then_inc(s_count, 1)
            pe.wait_ge(s_xn, 1)
            turn(0, s_turn)
            pe.wait_ge(s_branch, 1)

            def project_pair(i, last):
                products = 2 * 3 * KD * 3
                g = done = 0
                for u in range(2):
                    t = i * 2 + u
                    for m in range(3):
                        for n in range(KD * 3):
                            k = n // 3
                            if done * PER_PAIR >= g * products:
                                pe.wait_ge(s_weighted, i * PER_PAIR + g + 1)
                                edge_products(edge_bank[g % SLOTS], g % SLOTS, s_group)
                                g += 1
                            if n == 0:
                                if m == 0:
                                    pe.wait_ge(s_xT, t + 1)
                                if u == 0:
                                    pe.wait_ge(s_w_lo[m], 1)
                                pe.wait_ge((s_support, s_trans, s_gate_in)[m], t + 1)
                            done += 1
                            x_part, w_part = ((xT_hi, w_hi), (xT_hi, w_lo), (xT_lo, w_hi))[n % 3]
                            ins = pe.matmul(proj_bank[m][:, :], x_part[:, u, k * P:(k + 1) * P], w_part[:, m, k, :],
                                            start=(n == 0), stop=(n == KD * 3 - 1))
                        ins.then_inc(s_proj, 1)
                        if m == 1 and not (last and u):
                            pe.wait_ge(s_xn, t + 2)
                            turn(1 - u, s_turn)

            with pe.Fori(0, PAIRS - 1) as i:
                project_pair(i, False)
            project_pair(PAIRS - 1, True)

            for g in range(SLOTS):
                pe.wait_ge(s_weighted, GROUPS - SLOTS + g + 1)
                edge_products(edge_bank[g], g, s_group)

            pe.wait_ge(s_branch, 1)
            found = nc.values_load(strays_i[0:1, 0:1], engines=[PE], min_val=0, max_val=1)
            with pe.If(found == 0):
                pe.nop()
            with pe.Else():
                with pe.Fori(0, WINDOWS) as w:
                    with pe.Fori(0, GROUPS) as g:
                        pe.wait_ge(s_redo_onehot, w * GROUPS + g + 1)
                        edge_products(edge_bank[0], 0, s_redo_group)

            def turn_adj(t, first=False):
                pe.wait_ge(s_adj_block, t + 1)
                if not first:
                    pe.wait_ge(s_adjT, t)
                for k in range(NB):
                    ins = pe.transpose(adj_bank[k // 4][:, (k % 4) * P:(k % 4 + 1) * P],
                                       adj_block[:, k * P:(k + 1) * P], ident[:, :])
                    if k % 4 == 3 or k == NB - 1:
                        ins.then_inc(s_adj_turn, 1)

            def aggregate(t, u, logits_before=0, first=False):
                pe.wait_ge(s_adjT, t + 1)
                pe.wait_ge(s_agg_free, t + 1)
                for k in range(NB):
                    if k == NB - 3 and logits_before:
                        logits_of(t - 2, u, logits_before == 2)
                    if first:
                        if k < NB - 2:
                            pe.wait_ge(s_sup_lo[0], k + 1)
                        else:
                            pe.wait_ge(s_sup_lo[1], k - NB + 3)
                    for n, (a_part, s_part) in enumerate(((adjT_hi, sup_hi), (adjT_hi, sup_lo), (adjT_lo, sup_hi))):
                        ins = pe.matmul(agg_bank[u][:, :], a_part[:, u, k * P:(k + 1) * P], s_part[:, k, :],
                                        start=(k == 0 and n == 0), stop=(k == NB - 1 and n == 2))
                ins.then_inc(s_agg, 1)

            def turn_y(t, u):
                pe.wait_ge(s_y, t + 1)
                turn(u, s_turn2)

            def logits_of(t, u, placed):
                pe.wait_ge(s_yT, t + 1)
                if placed:
                    pe.wait_ge(s_placing, t)
                for k in range(KD):
                    ins = pe.matmul(misc_bank[:, 256 + u * E:256 + (u + 1) * E], yT[:, u, k * P:(k + 1) * P],
                                    wg_sb[:, k, :], start=(k == 0), stop=(k == KD - 1))
                ins.then_inc(s_logits, 1)

            def rank_tile_of(t, u, first):
                pe.wait_ge(s_chosen, t + 1)
                ins = pe.matmul(misc_bank[:, 320:320 + E], before[:, :], chosen[:, u, :], start=True, stop=first)
                if not first:
                    ins = pe.matmul(misc_bank[:, 320:320 + E], ones[:, :], chosen_sum[:, 1 - u, :],
                                    start=False, stop=True)
                ins.then_inc(s_rank, 1)

            pe.wait_ge(s_support, T + 1)
            pe.wait_ge(s_small, 16 * 6)
            turn_adj(0, first=True)
            turn_adj(1)
            aggregate(0, 0, first=True)
            turn_adj(2)
            aggregate(1, 1)
            turn_y(0, 0)
            turn_adj(3)
            aggregate(2, 0, 1)
            pe.wait_ge(s_ahead, 4)
            rank_tile_of(0, 0, True)
            turn_y(1, 1)
            with pe.Fori(1, PAIRS - 1) as i:
                for u in range(2):
                    t = i * 2 + u
                    turn_adj(t + 2)
                    aggregate(t + 1, 1 - u, 2)
                    turn_y(t, u)
                    rank_tile_of(t - 1, 1 - u, False)
            aggregate(T - 1, 1, 2)
            rank_tile_of(T - 3, 1, False)
            turn_y(T - 2, 0)
            logits_of(T - 2, 0, True)
            turn_y(T - 1, 1)
            rank_tile_of(T - 2, 0, False)
            logits_of(T - 1, 1, True)
            rank_tile_of(T - 1, 1, False)
            pe.wait_ge(s_placing, T)
            pe.matmul(misc_bank[:, 384:384 + E], ones[:, :], chosen_sum[:, 1, :], start=True, stop=True
                      ).then_inc(s_counts, 1)
            pe.wait_ge(s_over, 1)

            def turn_in(e, i, u):
                for c in range(CAP_TILES):
                    pe.wait_ge(s_got[u][c], i * 16 + 16)
                    turn_rows(y_in[:, u, c, :], in_bank[c], s_in_turned)

            def turn_rows(y_tile, to, done):
                for k in range(KD):
                    ins = pe.transpose(to[:, k * P:(k + 1) * P], y_tile[:, k * P:(k + 1) * P], ident[:, :])
                ins.then_inc(done, 1)

            def three(part, whole, left, right):
                for n, (a, b) in enumerate(((left[0], right[0]), (left[0], right[1]), (left[1], right[0]))):
                    ins = pe.matmul(whole, a, b, start=(part == "first" and n == 0),
                                    stop=(part == "last" and n == 2))
                return ins

            def which(k, n):
                return "first" if k == 0 else "last" if k == n - 1 else "middle"

            def up(u, done):
                for f in range(KF):
                    for k in range(KD):
                        ins = three(which(k, KD), up_bank[f][:, 0:CAP],
                                    [up_weights(w, u)[:, k, f * P:(f + 1) * P] for w in (ew_hi, ew_lo)],
                                    [y[:, k, :] for y in (yi_hi, yi_lo)])
                    ins.then_inc(done, 1)

            def down(e, u, c, done):
                for f in range(KF):
                    if c == 0:
                        pe.wait_ge(s_h, e * KF + f + 1)
                    ins = three(which(f, KF), down_bank[c][:, :],
                                [h[:, f, c * P:(c + 1) * P] for h in (h_hi, h_lo)],
                                [down_weights(w, u)[:, f, :] for w in (ew_hi, ew_lo)])
                ins.then_inc(done, 1)

            def expert(i, u, last):
                e = i * 2 + u
                pe.wait_ge(s_ew_lo, e * 2 + 1)
                pe.wait_ge(s_y_inT, e * CAP_TILES + CAP_TILES)
                up(u, s_up)
                if not last:
                    turn_in(e + 1, i + u, 1 - u)
                pe.wait_ge(s_ew_lo, e * 2 + 2)
                for c in range(CAP_TILES):
                    pe.wait_ge(s_taken, e * CAP_TILES + c + 1)
                    down(e, u, c, s_down)

            turn_in(0, 0, 0)
            with pe.Fori(0, E // 2 - 1) as i:
                expert(i, 0, False)
                expert(i, 1, False)
            expert(E // 2 - 1, 0, False)
            expert(E // 2 - 1, 1, True)

            def multiply_more():
                with pe.Fori(0, E) as e:
                    pe.wait_ge(s_more_expert, e * 32 + 32)
                    settle(pe)
                    with pe.Fori(0, MORE) as c:
                        n = e * MORE + c
                        pe.wait_ge(s_more_got, n * 16 + 16)
                        turn_rows(y_in[:, 0, 0, :], in_bank[0], s_more_turned)
                        pe.wait_ge(s_more_inT, n + 1)
                        for f in range(KF):
                            for k in range(KD):
                                ins = pe.matmul(up_bank[f][:, 0:P], up_weights(w_sb, 0)[:, k, f * P:(f + 1) * P],
                                                more_inT[:, k, :], start=(k == 0), stop=(k == KD - 1))
                        ins.then_inc(s_more_up, 1)
                        pe.wait_ge(s_more_h, n + 1)
                        pe.wait_ge(s_more_taken, n + 1)
                        for f in range(KF):
                            ins = pe.matmul(down_bank[0][:, :], hT[:, f, 0:P], down_weights(w_sb, 0)[:, f, :],
                                            start=(f == 0), stop=(f == KF - 1))
                        ins.then_inc(s_more_down, 1)

            pe.wait_ge(s_taken, E * CAP_TILES + CAP_TILES)
            beyond_share(pe, PE, multiply_more)

        @block.vector
        def _(dve):
            dve.sem_inc(s_trans, 1)
            dve.sem_inc(s_gate_in, 1)
            dve.sem_inc(s_trans_free, 1)
            dve.sem_inc(s_agg_free, 2)
            dve.sem_inc(s_x1y, 2)
            dve.sem_inc(s_taken, CAP_TILES)
            dve.sem_inc(s_more_taken, 1)
            dve.sem_inc(s_more_down, 1)
            dve.sem_inc(s_y_out_free, 1)

            chained = [0]

            def link(ins):
                chained[0] += 1
                ins.then_inc(s_chain, 1)
                dve.wait_ge(s_chain, chained[0])

            dve.wait_ge(s_edges, 64)
            dve.tensor_scalar(block_i[:, :], src_i[:, :], 7, None, ALU.logical_shift_right)
            dve.tensor_copy(dst_f, dst_i[:, :])
            link(dve.tensor_copy(below[:, 0:GROUPS], base_i[:, :]))
            dve.tensor_scalar(src_i[:, :], src_i[:, :], P - 1, None, ALU.bitwise_and)
            link(dve.tensor_tensor(col[:, :].rearrange("p (g j) -> p g j", j=GROUP),
                                   dst_f.rearrange("p (g j) -> p g j", j=GROUP),
                                   below[:, 0:GROUPS].unsqueeze(2).broadcast_to([P, GROUPS, GROUP]),
                                   ALU.subtract))
            dve.tensor_copy(src_lo, src_i[:, :])
            link(dve.tensor_scalar(block_col, block_i[:, :], float(WINDOW), None, ALU.mult))

            def columns():
                link(dve.tensor_scalar(outside[:, :], col[:, :], float(WINDOW), None, ALU.is_ge))
                link(dve.tensor_scalar(below[:, :], col[:, :], 0.0, None, ALU.is_lt))
                link(dve.tensor_tensor(outside[:, :], outside[:, :], below[:, :], ALU.add))

            columns()
            link(dve.tensor_tensor(col[:, :], col[:, :], block_col, ALU.add))
            dve.tensor_reduce(strays[:, :], outside[:, :], mybir.AxisListType.X, ALU.max).then_inc(s_strays, 1)
            link(dve.scalar_tensor_tensor(col[:, :], outside[:, :], float(2 * TOK), col[:, :], ALU.mult, ALU.add))

            for t in range(T):
                if t % PAIRS == 0:
                    dve.wait_ge(s_x[t // PAIRS], 16)
                ins = dve.bn_stats(stats[:, t, :], xs[:, t, :])
            link(ins)
            for t in range(T):
                ins = dve.bn_aggr(mv[:, t, :], stats[:, t, :])
            link(ins)
            dve.tensor_scalar(mv[:, :, 1], mv[:, :, 1], EPS, None, ALU.add).then_inc(s_var, 1)
            def onehots(slot, first):
                dve.tensor_tensor(rows[:, slot, :, :], iota[:, 0:P].unsqueeze(1).broadcast_to([P, GROUP, P]),
                                  now[:, 0, first:first + GROUP].unsqueeze(2).broadcast_to([P, GROUP, P]),
                                  ALU.is_equal)
                dve.tensor_tensor(cols[:, slot, :, :], iota[:, :].unsqueeze(1).broadcast_to([P, GROUP, COLS]),
                                  now[:, 2, first:first + GROUP].unsqueeze(2).broadcast_to([P, GROUP, COLS]),
                                  ALU.is_equal).then_inc(s_onehot, 1)

            def weighted_onehots():
                for j in range(GROUP):
                    dve.tensor_scalar(rows[:, 0, j, :], iota[:, 0:P], now[:, 0, j:j + 1], now[:, 1, j:j + 1],
                                      ALU.is_equal, ALU.mult)
                    ins = dve.tensor_scalar(cols[:, 0, j, :], iota[:, :], now[:, 2, j:j + 1], None, ALU.is_equal)
                ins.then_inc(s_redo_onehot, 1)

            def add_to_adj(bank, first, done):
                window = adj[:, :, bass.ds(first, WINDOW)]
                dve.tensor_tensor(window, bank[:, 0:COLS].rearrange("p (b w) -> p b w", w=WINDOW), window,
                                  ALU.add).then_inc(done, 1)

            def rest_of_xT(u, t):
                dve.wait_ge(s_xT_hi, t + 1)
                dve.tensor_tensor(xT_lo[:, u, :], turn_bank[u][:, :], xT_hi[:, u, :].bitcast(F32),
                                  ALU.subtract).then_inc(s_xT, 1)

            dve.wait_ge(s_const, 3)
            dve.wait_ge(s_adj_zero, 1)
            dve.sem_inc(s_flush, 1)

            def pick(of_pair, first, end):
                for a, values in enumerate((src_lo, edge_w_sb, col)):
                    ins = dve.tensor_copy(now[:, a, first * GROUP:end * GROUP],
                                          values[:, bass.ds((of_pair + first) * GROUP, (end - first) * GROUP)])
                ins.then_inc(s_now, 1)

            def firsts_of(n):
                return nc.values_load_multi_w_load_instructions(
                    base_i[0:1, bass.ds(n, SLOTS)], engines=[DVE], min_val=0, max_val=TOK,
                    skip_runtime_bounds_check_because="destinations are nodes")[1]

            def flush(n, g, first):
                dve.wait_ge(s_group, n + 1)
                dve.wait_ge(s_flush, n + 1)
                add_to_adj(edge_bank[g % SLOTS], first, s_flush)

            def pair_of_tiles(i, last):
                pick(i * PER_PAIR, SLOTS, PER_PAIR)

                def take_trans(u):
                    t = i * 2 + u
                    dve.wait_ge(s_proj, t * 3 + 2)
                    dve.wait_ge(s_trans_free, t + 1)
                    dve.tensor_tensor(trans, proj_bank[1][:, :], b_gnn_sb[:, 1, :], ALU.add).then_inc(s_trans, 1)

                def take_gate(u):
                    t = i * 2 + u
                    dve.wait_ge(s_proj, t * 3 + 3)
                    dve.tensor_tensor(tile(gate, t), proj_bank[2][:, :], b_gnn_sb[:, 2, :],
                                      ALU.add).then_inc(s_gate_in, 1)

                dve.wait_ge(s_now, i * 2 + 2)
                for g in range(PER_PAIR):
                    if g % SLOTS == 0:
                        firsts = firsts_of(i * PER_PAIR + g)
                    flush(i * PER_PAIR + g, g, firsts[g % SLOTS])
                    if g == PER_PAIR - SLOTS:
                        pick((i + 1) * PER_PAIR, 0, SLOTS)
                        dve.wait_ge(s_now, i * 2 + 3)
                    onehots(g % SLOTS, (g + SLOTS) % PER_PAIR * GROUP)
                    if g == 7:
                        take_trans(0)
                    if g == 8:
                        rest_of_xT(1, i * 2 + 1)
                    if g == 11:
                        take_gate(0)
                    if g == 18:
                        take_trans(1)
                    if g == 19 and not last:
                        rest_of_xT(0, i * 2 + 2)
                take_gate(1)

            pick(0, 0, SLOTS)
            dve.wait_ge(s_now, 1)
            onehots(0, 0)
            dve.wait_ge(s_std, 1)
            link(dve.reciprocal(norm[:, :, 0], std[:, :]))
            dve.scalar_tensor_tensor(norm[:, :, 1], mv[:, :, 0], -1.0, norm[:, :, 0],
                                     ALU.mult, ALU.mult).then_inc(s_norm, 1)
            dve.wait_ge(s_count, 1)
            dve.tensor_scalar(strays_i[:, :], count_bank[0:1, 0:1], 1.0, None, ALU.min).then_inc(s_branch, 1)
            for g in range(1, SLOTS):
                onehots(g, g * GROUP)
            rest_of_xT(0, 0)
            dve.wait_ge(s_filled, 16 * 3)
            dve.wait_ge(s_small, 16 * 6)
            with dve.Fori(0, PAIRS - 1) as i:
                pair_of_tiles(i, False)
            pair_of_tiles(PAIRS - 1, True)
            firsts = firsts_of(GROUPS - SLOTS)
            for g in range(SLOTS):
                flush(GROUPS - SLOTS + g, g, firsts[g])

            dve.wait_ge(s_branch, 1)
            found = nc.values_load(strays_i[0:1, 0:1], engines=[DVE], min_val=0, max_val=1)
            with dve.If(found == 0):
                dve.nop()
            with dve.Else():
                dve.wait_ge(s_flush, GROUPS + 1)
                dve.memset(adj[:, :, :], 0.0).then_inc(s_redo, 1)
                dve.wait_ge(s_redo, 1)
                with dve.Fori(0, WINDOWS) as w:
                    dve.tensor_copy(col[:, :], dst_f).then_inc(s_redo, 1)
                    dve.wait_ge(s_redo, w * 6 + 2)
                    dve.tensor_scalar(outside[:, :], col[:, :], float(WINDOW), None, ALU.is_ge)
                    dve.tensor_scalar(below[:, :], col[:, :], 0.0, None, ALU.is_lt).then_inc(s_redo, 1)
                    dve.wait_ge(s_redo, w * 6 + 3)
                    dve.tensor_tensor(outside[:, :], outside[:, :], below[:, :], ALU.add).then_inc(s_redo, 1)
                    dve.wait_ge(s_redo, w * 6 + 4)
                    dve.tensor_tensor(col[:, :], col[:, :], block_col, ALU.add).then_inc(s_redo, 1)
                    dve.wait_ge(s_redo, w * 6 + 5)
                    dve.scalar_tensor_tensor(col[:, :], outside[:, :], float(2 * TOK), col[:, :],
                                             ALU.mult, ALU.add)
                    dve.tensor_scalar(dst_f, dst_f, -float(WINDOW), None, ALU.add).then_inc(s_redo, 2)
                    dve.wait_ge(s_redo, w * 6 + 7)
                    settle(dve)
                    with dve.Fori(0, GROUPS) as g:
                        n = w * GROUPS + g
                        for a, edges in enumerate((src_lo, edge_w_sb[:, :], col[:, :])):
                            ins = dve.tensor_copy(now[:, a, 0:GROUP], edges[:, bass.ds(g * GROUP, GROUP)])
                        ins.then_inc(s_redo_copy, 1)
                        dve.wait_ge(s_redo_copy, n + 1)
                        weighted_onehots()
                        dve.wait_ge(s_redo_group, n + 1)
                        add_to_adj(edge_bank[0], w * WINDOW, s_redo_flush)
                        dve.wait_ge(s_redo_flush, n + 1)

            def stage(t):
                dve.tensor_copy(adj_block[:, :], adj[:, bass.ds(t, 1), 0:TOK].rearrange("p a n -> p (a n)")
                                ).then_inc(s_adj_block, 1)

            def rest_of_adjT(t, u):
                for c in range(3):
                    n = min(4, NB - 4 * c)
                    part = slice(4 * c * P, (4 * c + n) * P)
                    dve.wait_ge(s_adjT_hi, t * 3 + c + 1)
                    ins = dve.tensor_tensor(adjT_lo[:, u, part], adj_bank[c][:, 0:n * P],
                                            adjT_hi[:, u, part].bitcast(F32), ALU.subtract)
                ins.then_inc(s_adjT, 1)

            dve.wait_ge(s_flush, GROUPS + 1)
            stage(0)
            for k in range(NB - 2, NB):
                dve.wait_ge(s_sup_hi, k // 2 + 1)
                split_support(dve, k, s_sup_lo[1])
            dve.wait_ge(s_adj_turn, 3)
            stage(1)
            rest_of_adjT(0, 0)
            rest_of_adjT(1, 1)

            def choose(t, u, first, last):
                step = t * 8
                dve.wait_ge(s_logits, t + 1)
                dve.tensor_tensor(logits[:, u, :], misc_bank[:, 256 + u * E:256 + (u + 1) * E], bg_sb[:, :],
                                  ALU.add).then_inc(s_pick, 1)
                dve.wait_ge(s_pick, step + 1)
                settle(dve)
                dve.max(best[:, u, :], logits[:, u, :]).then_inc(s_pick, 1)
                dve.wait_ge(s_pick, step + 2)
                settle(dve)
                dve.max_index(best_i[:, u, :], best[:, u, :], logits[:, u, :]).then_inc(s_pick, 1)
                dve.tensor_tensor(odds[:, u:u + 1], best[:, u, 1:2], best[:, u, 0:1], ALU.subtract).then_inc(s_gap, 1)
                dve.wait_ge(s_pick, step + 3)
                dve.tensor_copy(best_f[:, u, :], best_i[:, u, 0:TOP_K]).then_inc(s_pick, 1)
                dve.wait_ge(s_pick, step + 4)
                dve.tensor_tensor(hit[:, u, :, :], iota[:, 0:E].unsqueeze(1).broadcast_to([P, TOP_K, E]),
                                  best_f[:, u, :].unsqueeze(2).broadcast_to([P, TOP_K, E]),
                                  ALU.is_equal).then_inc(s_pick, 1)
                dve.wait_ge(s_pick, step + 5)
                dve.tensor_tensor(chosen[:, u, :], hit[:, u, 0, :], hit[:, u, 1, :], ALU.add).then_inc(s_pick, 1)
                dve.wait_ge(s_pick, step + 6)
                if last:
                    dve.tensor_scalar(chosen[:, u, :], chosen[:, u, :], real[:, :], None, ALU.mult).then_inc(s_pick, 1)
                    dve.wait_ge(s_pick, step + 7)
                if first:
                    dve.tensor_copy(chosen_sum[:, u, :], chosen[:, u, :]).then_inc(s_chosen, 1)
                else:
                    dve.wait_ge(s_chosen, t)
                    dve.tensor_tensor(chosen_sum[:, u, :], chosen_sum[:, 1 - u, :], chosen[:, u, :],
                                      ALU.add).then_inc(s_chosen, 1)
                if not last:
                    dve.sem_inc(s_pick, 2)

            def place(i, u, saved, last):
                t = i * 2 + u
                step = t * 5
                if saved:
                    dve.wait_ge(s_route_saved[u], i * (16 * TOP_K))
                dve.wait_ge(s_rank, t + 1)
                dve.tensor_tensor(hit_rank[:, u, :, :], hit[:, u, :, :],
                                  misc_bank[:, 320:320 + E].unsqueeze(1).broadcast_to([P, TOP_K, E]),
                                  ALU.mult).then_inc(s_placing, 1)
                dve.tensor_scalar(first_col[:, u, :], best_f[:, u, :], float(T), None, ALU.mult)
                dve.tensor_copy(route[:, u, :, 0], token_i[:, bass.ds(t, 1)].broadcast_to([P, TOP_K]))
                dve.wait_ge(s_odds, t + 1)
                dve.tensor_scalar(odds1[:, u:u + 1], odds[:, u:u + 1], 1.0, None, ALU.add).then_inc(s_place, 1)
                dve.wait_ge(s_place, step + 1)
                dve.tensor_reduce(rank[:, u, :], hit_rank[:, u, :, :], mybir.AxisListType.X, ALU.add)
                dve.reciprocal(route_score[:, u, 0, 1:2], odds1[:, u:u + 1]).then_inc(s_place, 1)
                dve.wait_ge(s_place, step + 2)
                dve.tensor_tensor(route_score[:, u, 1, 1:2], route_score[:, u, 0, 1:2], odds[:, u:u + 1], ALU.mult)
                dve.tensor_copy(rank_i[:, u, :], rank[:, u, :]).then_inc(s_place, 1)
                dve.wait_ge(s_place, step + 3)
                dve.scalar_tensor_tensor(row[:, u, :], rank[:, u, :], float(ROUTES), first_col[:, u, :],
                                         ALU.mult, ALU.add)
                dve.tensor_scalar(rank_tile_i[:, u, :], rank_i[:, u, :], 7, None,
                                  ALU.logical_shift_right).then_inc(s_place, 1)
                dve.wait_ge(s_place, step + 4)
                dve.tensor_copy(rank_tile[:, u, :], rank_tile_i[:, u, :]).then_inc(s_place, 1)
                dve.wait_ge(s_place, step + 5)
                if last:
                    link_last = dve.scalar_tensor_tensor(row[:, u, :], rank_tile[:, u, :], -float(P * ROUTES - 1),
                                                         row[:, u, :], ALU.mult, ALU.add)
                    link_last.then_inc(s_place, 1)
                    dve.wait_ge(s_place, T * 5 + 1)
                    dve.scalar_tensor_tensor(row_i[:, u, :, 0], row[:, u, :], real[:, :], unreal_row[:, :],
                                             ALU.mult, ALU.add).then_inc(s_routed, 1)
                else:
                    dve.scalar_tensor_tensor(row_i[:, u, :, 0], rank_tile[:, u, :], -float(P * ROUTES - 1),
                                             row[:, u, :], ALU.mult, ALU.add).then_inc(s_routed, 1)

            def finish(i, u, more, now_place, now_choose):
                t = i * 2 + u
                xt, gt = tile(xs, t), tile(gate, t)
                x1t = x1[:, u, :]
                dve.wait_ge(s_agg, t + 1)
                dve.wait_ge(s_x1y, t + 1)
                dve.tensor_tensor(x1t, agg_bank[u][:, :], b_gnn_sb[:, 0, :], ALU.add).then_inc(s_agg_free, 1)
                dve.wait_ge(s_agg_free, t + 3)
                dve.scalar_tensor_tensor(x1t, x1t, 0.0, gt, ALU.max, ALU.mult).then_inc(s_relu, 1)
                dve.wait_ge(s_relu, t + 1)
                dve.tensor_tensor(x1t, xt, x1t, ALU.add).then_inc(s_x1, 1)
                dve.wait_ge(s_x1, t + 1)
                dve.bn_stats(stats[:, u, :], x1t).then_inc(s_ln, 1)
                dve.wait_ge(s_ln, t * 2 + 1)
                settle(dve)
                dve.bn_aggr(mv2[:, u, :], stats[:, u, :]).then_inc(s_ln, 1)
                dve.wait_ge(s_ln, t * 2 + 2)
                dve.tensor_scalar(mv2[:, u, 1:2], mv2[:, u, 1:2], EPS, None, ALU.add).then_inc(s_var2, 1)
                if now_place:
                    place(i - 1, u, now_place == 2, False)
                dve.wait_ge(s_std2, t + 1)
                dve.reciprocal(norm2[:, u, 0:1], std2[:, u:u + 1]).then_inc(s_rec2, 1)
                dve.wait_ge(s_rec2, t + 1)
                dve.scalar_tensor_tensor(norm2[:, u, 1:2], mv2[:, u, 0:1], -1.0, norm2[:, u, 0:1],
                                         ALU.mult, ALU.mult).then_inc(s_norm2, 1)
                if more:
                    rest_of_adjT(t + 2, u)
                if now_choose:
                    choose(t - 1, 1 - u, now_choose == 1, False)

            dve.wait_ge(s_ahead, 4)
            dve.wait_ge(s_trans_free, T + 1)
            finish(0, 0, True, 0, 0)
            finish(0, 1, True, 0, 1)
            finish(1, 0, True, 1, 2)
            finish(1, 1, True, 1, 2)
            with dve.Fori(2, PAIRS - 1) as i:
                for u in range(2):
                    finish(i, u, True, 2, 2)
            finish(PAIRS - 1, 0, False, 2, 2)
            finish(PAIRS - 1, 1, False, 2, 2)
            place(PAIRS - 1, 0, True, False)
            choose(T - 1, 1, False, True)
            place(PAIRS - 1, 1, True, True)

            dve.wait_ge(s_counts, 1)
            link(dve.tensor_reduce(most[:, :], misc_bank[0:1, 384:384 + E], mybir.AxisListType.X, ALU.max))
            dve.tensor_scalar(over_i[:, :], most[:, :], float(CAP), None, ALU.is_gt).then_inc(s_over, 1)

            def add_b2(e, bank_c, out_c, done):
                dve.tensor_tensor(out_c, bank_c[:, :], b2_sb[:, bass.ds(e, 1), :].rearrange("p a d -> p (a d)"),
                                  ALU.add).then_inc(done, 1)

            def scale(column, out_c, done):
                dve.tensor_scalar(out_c, out_c, table_score[:, bass.ds(column, 1), 1], None,
                                  ALU.mult).then_inc(done, 1)

            def split_weights_lo(e, u, half):
                dve.wait_ge(s_ew_hi, e * 2 + (1 if half == of_up else 2))
                dve.tensor_tensor(ew_lo[:, u, half], w_sb[:, u, half], ew_hi[:, u, half].bitcast(F32),
                                  ALU.subtract).then_inc(s_ew_lo, 1)

            def rest_of_rows(e):
                for c in range(CAP_TILES):
                    tokens = slice(c * P, (c + 1) * P)
                    dve.wait_ge(s_y_hi, e * CAP_TILES + c + 1)
                    dve.tensor_tensor(yi_lo[:, :, tokens], in_bank[c][:, :].rearrange("p (k n) -> p k n", k=KD),
                                      yi_hi[:, :, tokens].bitcast(F32), ALU.subtract).then_inc(s_y_inT, 1)

            def expert(i, u, last):
                e = i * 2 + u
                if not last:
                    split_weights_lo(e + 1, 1 - u, of_up)
                for f in range(KF):
                    dve.wait_ge(s_h_hi, e * KF + f + 1)
                    dve.tensor_tensor(h_lo[:, f, :], hT[:, f, :], h_hi[:, f, :].bitcast(F32),
                                      ALU.subtract).then_inc(s_h, 1)
                if not last:
                    rest_of_rows(e + 1)
                    split_weights_lo(e + 1, 1 - u, of_down)
                dve.wait_ge(s_y_out_free, e + 1)
                for c in range(CAP_TILES):
                    dve.wait_ge(s_down, e * CAP_TILES + c + 1)
                    add_b2(e, down_bank[c], y_out[:, u, c, :], s_taken)

            split_weights_lo(0, 0, of_up)
            split_weights_lo(0, 0, of_down)
            rest_of_rows(0)
            dve.wait_ge(s_table, 16)
            dve.wait_ge(s_b2, 16)
            with dve.Fori(0, E // 2 - 1) as i:
                expert(i, 0, False)
                expert(i, 1, False)
            expert(E // 2 - 1, 0, False)
            expert(E // 2 - 1, 1, True)

            def scale_more():
                for u in range(2):
                    dve.wait_ge(s_added[u], 16 * CAP_TILES * (E // 2))
                with dve.Fori(0, E) as e:
                    with dve.Fori(0, MORE) as c:
                        n = e * MORE + c
                        dve.wait_ge(s_more_down, n + 2)
                        add_b2(e, down_bank[0], y_out[:, 0, 0, :], s_more_taken)
                        dve.wait_ge(s_more_taken, n + 2)
                        scale(e * T + c + CAP_TILES, y_out[:, 0, 0, :], s_more_scaled)

            beyond_share(dve, DVE, scale_more)


def kernel(x, src, dst, edge_weight, L0_gnn_w1, L0_gnn_w2, L0_gnn_w3, L0_gnn_b1, L0_gnn_b2, L0_gnn_b3,
           L0_ffn_Wg, L0_ffn_bg, L0_ffn_W1, L0_ffn_b1, L0_ffn_W2, L0_ffn_b2):
    from concourse import bacc
    from concourse.bass_utils import run_bass_kernel_spmd

    x, src, dst, edge_weight = (np.asarray(a) for a in (x, src, dst, edge_weight))
    n, d = x.shape
    tiles, pairs, per_pair, groups = split_shapes(n, len(src))
    slots = groups * GROUP * P
    more = slots - len(src)

    def by_tile(a):
        return np.ascontiguousarray(a.reshape(groups * GROUP, P).T)

    src_p = np.pad(src, (0, more), mode="edge")
    dst_p = np.pad(dst, (0, more), mode="edge")
    e, _, f = np.shape(L0_ffn_W1)
    arrays = {
        "x": np.pad(x, ((0, tiles * P - n), (0, 0))),
        "src": by_tile(src_p),
        "dst": by_tile(dst_p),
        "first_dst": np.ascontiguousarray(dst_p[:: GROUP * P][None, :]),
        "edge_w": by_tile(np.pad(edge_weight, (0, more))),
        "w_gnn": np.stack([L0_gnn_w1, L0_gnn_w2, L0_gnn_w3]),
        "b_gnn": np.stack([L0_gnn_b1, L0_gnn_b2, L0_gnn_b3]),
        "wg": np.asarray(L0_ffn_Wg),
        "bg": np.asarray(L0_ffn_bg)[None, :],
        "w1": np.asarray(L0_ffn_W1),
        "b1": np.ascontiguousarray(np.asarray(L0_ffn_b1).reshape(e, f // P, P).transpose(2, 1, 0)),
        "w2": np.asarray(L0_ffn_W2),
        "b2": np.ascontiguousarray(np.asarray(L0_ffn_b2).reshape(1, -1)),
    }
    nc = bacc.Bacc("TRN2", target_bir_lowering=False, num_devices=1, dynamic_dma_scratch_size=12288)
    args = {
        name: nc.dram_tensor(f"in_{name}", a.shape, mybir.dt.from_np(a.dtype), kind="ExternalInput").ap()
        for name, a in arrays.items()
    }
    rows = (tiles + CAP_TILES) * P
    out = nc.dram_tensor("out", (rows, d), F32, kind="ExternalOutput").ap()
    y_rows = nc.dram_tensor("y_rows", (rows, d), F32, kind="Internal").ap()
    routes = nc.dram_tensor("routes", (P * e * tiles + P * TOP_K, 2), I32, kind="Internal").ap()
    gnn_moe_layer(nc, out=out, y_rows=y_rows, routes=routes, n_nodes=n, **args)
    r = run_bass_kernel_spmd(nc, [{f"in_{name}": a for name, a in arrays.items()}], core_ids=[0])
    return r.results[0]["out"][:n]
```
